# Optimizing a Trainium2 kernel written in Bass

```python
import numpy as np
import jax
import jax.numpy as jnp

def _softmax(x, axis=-1):
    return jax.nn.softmax(x, axis=axis)

def _gelu(x):
    return jax.nn.gelu(x, approximate=True)

def _silu(x):
    return jax.nn.silu(x)

def _sigmoid(x):
    return jax.nn.sigmoid(x)

def _layernorm(x, axis=-1, eps=1e-05):
    m = jnp.mean(x, axis=axis, keepdims=True)
    v = jnp.var(x, axis=axis, keepdims=True)
    return (x - m) / jnp.sqrt(v + eps)

def _scatter_add(tgt, idx, src, axis=0):
    return tgt.at[idx].add(src)

def _segment_sum(src, seg, n):
    return jax.ops.segment_sum(src, seg, n)
kernel_name = 'mk_xattn_seq_d1_seqx_r4_d19f26'

def setup_inputs(seed: int=0):
    np.random.seed(seed)
    _w = jnp.asarray

    def _rec_inputs():
        import jax
        import jax.numpy as jnp
        _rk = jax.random.key(seed)
        x = 7.22e-05 + 1 * jax.random.normal(jax.random.fold_in(_rk, 1), (32, 256, 256), jnp.float32)
        _lenS = 256 - jax.random.randint(jax.random.fold_in(_rk, 7), (32,), 0, max(1, 256 // 4) + 1, jnp.int32)
        _lenS2 = 120 - jax.random.randint(jax.random.fold_in(_rk, 8), (32,), 0, max(1, 120 // 4) + 1, jnp.int32)
        _ctx_768P = jax.random.normal(jax.random.fold_in(_rk, 11), (32, 16, 192), jnp.float32)
        _ctx_768c = jax.random.dirichlet(jax.random.fold_in(_rk, 511), 0.3 * jnp.ones((16,), jnp.float32), (32, 120))
        _ctx_768t = jnp.einsum('bsk,bkd->bsd', _ctx_768c, _ctx_768P)
        _ctx_768t = _ctx_768t * jax.lax.rsqrt(jnp.mean(jnp.square(_ctx_768t)) + 1e-12) * 0.953939
        ctx_768 = 0.00272024 + 0.999456 * (_ctx_768t + 0.3 * jax.random.normal(jax.random.fold_in(_rk, 611), (32, 120, 192), jnp.float32))
        return (x, ctx_768)
    x, ctx_768 = _rec_inputs()

    def _L0_xattn_setup():
        import jax, jax.numpy as jnp
        import numpy as np
        N_HEADS = 16
        D_HEAD = 64
        D_MODEL = 256
        D_COND = 192
        D_FF = 4 * D_MODEL
        EPS = 1e-05

        def _layernorm(x, g, b):
            m = jnp.mean(x, axis=-1, keepdims=True)
            v = jnp.mean(jnp.square(x - m), axis=-1, keepdims=True)
            return (x - m) * jax.lax.rsqrt(v + EPS) * g + b

        def _attention(x, cond, wq, wk, wv, wo, bo):
            B, Sq, _ = x.shape
            Sk = cond.shape[1]
            q = (x @ wq).reshape(B, Sq, N_HEADS, D_HEAD)
            k = (cond @ wk).reshape(B, Sk, N_HEADS, D_HEAD)
            v = (cond @ wv).reshape(B, Sk, N_HEADS, D_HEAD)
            scale = D_HEAD ** (-0.5)
            attn = jnp.einsum('bqhd,bkhd->bhqk', q, k) * scale
            attn = jax.nn.softmax(attn, axis=-1)
            out = jnp.einsum('bhqk,bkhd->bqhd', attn, v).reshape(B, Sq, N_HEADS * D_HEAD)
            return out @ wo + bo
        key = jax.random.key(seed)
        ks = jax.random.split(key, 16)
        d_attn = N_HEADS * D_HEAD
        s = lambda fan_in: fan_in ** (-0.5)
        inp = {'x': jax.random.normal(ks[0], (8, 256, D_MODEL), jnp.float32), 'cond': jax.random.normal(ks[1], (8, 77, D_COND), jnp.float32), 'wq1': jax.random.normal(ks[2], (D_MODEL, d_attn), jnp.float32) * s(D_MODEL), 'wk1': jax.random.normal(ks[3], (D_MODEL, d_attn), jnp.float32) * s(D_MODEL), 'wv1': jax.random.normal(ks[4], (D_MODEL, d_attn), jnp.float32) * s(D_MODEL), 'wo1': jax.random.normal(ks[5], (d_attn, D_MODEL), jnp.float32) * s(d_attn), 'bo1': jnp.zeros((D_MODEL,), jnp.float32), 'g1': jnp.ones((D_MODEL,), jnp.float32), 'b1': jnp.zeros((D_MODEL,), jnp.float32), 'wq2': jax.random.normal(ks[6], (D_MODEL, d_attn), jnp.float32) * s(D_MODEL), 'wk2': jax.random.normal(ks[7], (D_COND, d_attn), jnp.float32) * s(D_COND), 'wv2': jax.random.normal(ks[8], (D_COND, d_attn), jnp.float32) * s(D_COND), 'wo2': jax.random.normal(ks[9], (d_attn, D_MODEL), jnp.float32) * s(d_attn), 'bo2': jnp.zeros((D_MODEL,), jnp.float32), 'g2': jnp.ones((D_MODEL,), jnp.float32), 'b2': jnp.zeros((D_MODEL,), jnp.float32), 'w_ff1': jax.random.normal(ks[10], (D_MODEL, 2 * D_FF), jnp.float32) * s(D_MODEL), 'b_ff1': jnp.zeros((2 * D_FF,), jnp.float32), 'w_ff2': jax.random.normal(ks[11], (D_FF, D_MODEL), jnp.float32) * s(D_FF), 'b_ff2': jnp.zeros((D_MODEL,), jnp.float32), 'g3': jnp.ones((D_MODEL,), jnp.float32), 'b3': jnp.zeros((D_MODEL,), jnp.float32)}
        return inp
    _L0_xattn_all = _L0_xattn_setup()
    _L0_xattn_in = {k: v for k, v in _L0_xattn_all.items() if k in ('wq1', 'wk1', 'wv1', 'wo1', 'bo1', 'g1', 'b1', 'wq2', 'wk2', 'wv2', 'wo2', 'bo2', 'g2', 'b2', 'w_ff1', 'b_ff1', 'w_ff2', 'b_ff2', 'g3', 'b3')}
    del _L0_xattn_all
    return {'x': x, 'ctx_768': ctx_768, 'L0_xattn_wq1': _L0_xattn_in['wq1'], 'L0_xattn_wk1': _L0_xattn_in['wk1'], 'L0_xattn_wv1': _L0_xattn_in['wv1'], 'L0_xattn_wo1': _L0_xattn_in['wo1'], 'L0_xattn_bo1': _L0_xattn_in['bo1'], 'L0_xattn_g1': _L0_xattn_in['g1'], 'L0_xattn_b1': _L0_xattn_in['b1'], 'L0_xattn_wq2': _L0_xattn_in['wq2'], 'L0_xattn_wk2': _L0_xattn_in['wk2'], 'L0_xattn_wv2': _L0_xattn_in['wv2'], 'L0_xattn_wo2': _L0_xattn_in['wo2'], 'L0_xattn_bo2': _L0_xattn_in['bo2'], 'L0_xattn_g2': _L0_xattn_in['g2'], 'L0_xattn_b2': _L0_xattn_in['b2'], 'L0_xattn_w_ff1': _L0_xattn_in['w_ff1'], 'L0_xattn_b_ff1': _L0_xattn_in['b_ff1'], 'L0_xattn_w_ff2': _L0_xattn_in['w_ff2'], 'L0_xattn_b_ff2': _L0_xattn_in['b_ff2'], 'L0_xattn_g3': _L0_xattn_in['g3'], 'L0_xattn_b3': _L0_xattn_in['b3']}

def reference(x, ctx_768, L0_xattn_wq1, L0_xattn_wk1, L0_xattn_wv1, L0_xattn_wo1, L0_xattn_bo1, L0_xattn_g1, L0_xattn_b1, L0_xattn_wq2, L0_xattn_wk2, L0_xattn_wv2, L0_xattn_wo2, L0_xattn_bo2, L0_xattn_g2, L0_xattn_b2, L0_xattn_w_ff1, L0_xattn_b_ff1, L0_xattn_w_ff2, L0_xattn_b_ff2, L0_xattn_g3, L0_xattn_b3):
    import jax
    import jax.numpy as jnp

    def _L0_xattn_ref(x, cond, wq1, wk1, wv1, wo1, bo1, g1, b1, wq2, wk2, wv2, wo2, bo2, g2, b2, w_ff1, b_ff1, w_ff2, b_ff2, g3, b3):
        import jax, jax.numpy as jnp
        import numpy as np
        N_HEADS = 16
        D_HEAD = 64
        D_MODEL = 256
        D_COND = 192
        D_FF = 4 * D_MODEL
        EPS = 1e-05

        def _layernorm(x, g, b):
            m = jnp.mean(x, axis=-1, keepdims=True)
            v = jnp.mean(jnp.square(x - m), axis=-1, keepdims=True)
            return (x - m) * jax.lax.rsqrt(v + EPS) * g + b

        def _attention(x, cond, wq, wk, wv, wo, bo):
            B, Sq, _ = x.shape
            Sk = cond.shape[1]
            q = (x @ wq).reshape(B, Sq, N_HEADS, D_HEAD)
            k = (cond @ wk).reshape(B, Sk, N_HEADS, D_HEAD)
            v = (cond @ wv).reshape(B, Sk, N_HEADS, D_HEAD)
            scale = D_HEAD ** (-0.5)
            attn = jnp.einsum('bqhd,bkhd->bhqk', q, k) * scale
            attn = jax.nn.softmax(attn, axis=-1)
            out = jnp.einsum('bhqk,bkhd->bqhd', attn, v).reshape(B, Sq, N_HEADS * D_HEAD)
            return out @ wo + bo
        h = _layernorm(x, g1, b1)
        x = _attention(h, h, wq1, wk1, wv1, wo1, bo1) + x
        h = _layernorm(x, g2, b2)
        x = _attention(h, cond, wq2, wk2, wv2, wo2, bo2) + x
        h = _layernorm(x, g3, b3)
        proj = h @ w_ff1 + b_ff1
        a, gate = jnp.split(proj, 2, axis=-1)
        ff = a * jax.nn.gelu(gate, approximate=False) @ w_ff2 + b_ff2
        return ff + x
    x = _L0_xattn_ref(x, ctx_768, L0_xattn_wq1, L0_xattn_wk1, L0_xattn_wv1, L0_xattn_wo1, L0_xattn_bo1, L0_xattn_g1, L0_xattn_b1, L0_xattn_wq2, L0_xattn_wk2, L0_xattn_wv2, L0_xattn_wo2, L0_xattn_bo2, L0_xattn_g2, L0_xattn_b2, L0_xattn_w_ff1, L0_xattn_b_ff1, L0_xattn_w_ff2, L0_xattn_b_ff2, L0_xattn_g3, L0_xattn_b3)
    return x

_drawn_inputs = setup_inputs


def setup_inputs(seed=0):
    import zlib

    import numpy as np

    out = dict(_drawn_inputs(seed))
    spreads = {'L0_xattn_bo1': (0.0, 0.1),
     'L0_xattn_g1': (1.0, 0.2),
     'L0_xattn_b1': (0.0, 0.1),
     'L0_xattn_bo2': (0.0, 0.1),
     'L0_xattn_g2': (1.0, 0.2),
     'L0_xattn_b2': (0.0, 0.402),
     'L0_xattn_b_ff1': (0.0, 0.1),
     'L0_xattn_b_ff2': (0.0, 0.1),
     'L0_xattn_g3': (1.0, 0.2),
     'L0_xattn_b3': (0.0, 0.1)}
    factors = {}
    for name, (base, spread) in spreads.items():
        noise = np.random.default_rng([zlib.crc32(name.encode()), seed]).standard_normal(out[name].shape)
        drawn = base * np.exp(spread * noise) if base else spread * noise
        out[name] = jnp.asarray(drawn.astype(out[name].dtype))
    for name, factor in factors.items():
        out[name] = (out[name] * factor).astype(out[name].dtype)
    return out
```

```python
from contextlib import ExitStack

import concourse.bass as bass
from concourse import mybir

ALU = mybir.AluOpType
ACT = mybir.ActivationFunctionType
AX = mybir.AxisListType
F32, F16, F32R, I32 = mybir.dt.float32, mybir.dt.float16, mybir.dt.float32r, mybir.dt.int32

P = 128
HEADS, DH = 16, 64
PAIRS = HEADS // 2
EPS = 1e-5
SLOTS = 2

BOUND = 14
Q_SHIFT = 18
C_SHIFT = 22
FLOOR = 2.0 ** -20
EXPONENT = 0x7F800000

WEIGHTS = ["wq1", "wk1", "wv1", "wo1", "wq2", "wk2", "wv2", "wo2", "ff1"]
COL = {n: i for i, n in enumerate(WEIGHTS + ["ctx", "h1", "h2", "h3", "b1", "b2", "b3"])}
NCOL = 16


def make_order():
    A, B = 0, 1
    order = [("stats", A, 1), ("stats", B, 1), ("turn", A, 1)]
    order += [("proj", A, "q1", 0), ("proj", A, "k1", 0), ("scores", 0), ("exp", 0), ("scores", 1), ("exp", 1),
              ("proj", A, "q1", 1), ("proj", A, "k1", 1), ("turn", B, 1)]

    def proj(s, *names):
        return [("proj", s, n[:2], int(n[2])) for n in names]

    def out(s, n):
        return [("out", s, n, 0), ("out", s, n, 1), ("stats", s, n + 1)]

    fills = {
        0: proj(A, "v10", "v12"), 1: proj(A, "q12", "k12"), 2: proj(A, "q13", "k13"), 3: proj(A, "v11", "v13"),
        4: proj(B, "q10", "k10"), 5: proj(B, "q11", "k11"), 6: proj(B, "v10", "v12"), 7: proj(B, "q12", "k12"),
        8: proj(B, "q13", "k13"), 9: out(A, 1), 10: proj(B, "v11", "v13"),
        11: [("ctx", A), ("turn", A, 2)], 12: proj(A, "k20", "q20"), 13: proj(A, "v20", "q21"),
        14: proj(A, "k21", "q22"), 15: proj(A, "v21", "q23"), 16: [("ctx", B)] + proj(B, "k20"),
        17: out(B, 1), 18: proj(B, "v20"), 19: [("turn", B, 2)] + proj(B, "q20"), 20: proj(B, "q21", "v21"),
        21: proj(B, "k21"), 22: proj(B, "q22"), 23: proj(B, "q23"), 25: out(A, 2), 27: [("turn", A, 3)],
    }
    last = 4 * PAIRS - 1
    for p in range(last + 1):
        order.append(("norm", p))
        if p + 2 <= last:
            order.append(("scores", p + 2))
        order += fills.get(p, [])
        order.append(("turn_probs", p))
        if p + 2 <= last:
            order.append(("exp", p + 2))
        order.append(("split_probs", p))
        if p >= 1:
            order.append(("mix", p - 1))
    order.append(("mix", last))
    order += out(B, 2)

    def feed(s):
        steps = []
        for j in range(8 + 2):
            if j < 8:
                steps.append(("ff1", s, j))
            if j >= 2:
                steps.append(("ff2", s, j - 2))
        return steps + [("finish", s)]

    return order + feed(A) + [("turn", B, 3)] + feed(B)


ORDER = make_order()

IN_GROUPS = ("turn", "proj", "ctx", "mix", "out", "ff1")
GROUP = {step: i for i, step in enumerate(x for x in ORDER if x[0] in IN_GROUPS)}
NGROUP = len(GROUP)
HIGH = {step: i for i, step in enumerate(x for x in ORDER if x[0] in ("proj", "mix"))}
NHIGH = len(HIGH)
STATS = {step[1:]: i for i, step in enumerate(x for x in ORDER if x[0] == "stats")}
TURNS = {step[1:]: i for i, step in enumerate(x for x in ORDER if x[0] == "turn")}
CTXS = {step[1]: i for i, step in enumerate(x for x in ORDER if x[0] == "ctx")}
TILES = {step[1:]: i for i, step in enumerate(x for x in ORDER if x[0] == "ff1")}
NPAIR = 4 * PAIRS
NLN = len(STATS)
NTILE = len(TILES)
assert NGROUP % 2 == 0 and NPAIR % 2 == 0 and NTILE % 4 == 0


def of_pair(p):
    return p // PAIRS % 2, p // (2 * PAIRS) + 1, p % PAIRS


def units(p):
    return [2 * p, 2 * p + 1] if p < 2 * PAIRS else [2 * PAIRS + p]


NUNIT = units(NPAIR - 1)[-1] + 1
assert NUNIT % 4 == 0


def bass_xattn_block(nc, x, ctx, w, g, b, bo, b_ff1, out):
    NB, S, D = x.shape
    SK, DC = ctx.shape[1], ctx.shape[2]
    DA = HEADS * DH
    FF = w["ff2"].shape[0]
    KT, TT, AT = D // P, S // P, DA // P
    FT = FF // P
    KC = DC // 2
    TURNS_OF_LOOP = NB // SLOTS
    SCALE = DH ** -0.5
    assert D == 256 and S == 256 and SK <= P and KC <= P and AT == PAIRS and FT == 8

    with ExitStack() as stack:
        def sb(name, shape, dt):
            return stack.enter_context(nc.sbuf_tensor(name, shape, dt))

        def sem(name):
            return stack.enter_context(nc.semaphore(name))

        kp = {n: KC if n in ("wk2", "wv2") else P for n in WEIGHTS}
        shape = {n: [2, AT, D] if n in ("wo1", "wo2") else [2, 2, 2 * FF] if n == "ff1" else [2, 2, DA] for n in WEIGHTS}
        wsb = {n: sb(n, [P] + shape[n], F16) for n in WEIGHTS}
        w2sb = [sb(f"w2_{i}", [P, FT, D], F32R) for i in ("high", "low")]
        ident = sb("ident", [P, P], F32)
        ones = sb("ones", [NCOL, P], F32)
        half = sb("half", [P, TT], F32)
        bias_rows = sb("bias_rows", [P, 3, D], F32)
        NVEC = 3 * 2 * KT + 2 * FT
        vec_rows = sb("vec_rows", [NVEC, P], F32)
        vecs = sb("vecs", [P, NVEC], F32)
        gains = vecs[:, 0:6 * KT].rearrange("p (i c k) -> p i c k", i=3, c=2)
        ffb = vecs[:, 6 * KT:NVEC]
        gains_s = sb("gains_s", [P, 3, 2, KT], F32)
        ffb_a = sb("ffb_a", [P, FT], F32)
        largest = sb("largest", [P, NCOL], F32)
        top = sb("top", [NCOL, 1], F32)
        diag = sb("diag", [NCOL, NCOL], F32)
        bound = sb("bound", [P, NCOL], F32)
        power = sb("power", [P, NCOL], F32)
        up = sb("up", [P, NCOL], F32)
        down = sb("down", [P, NCOL], F32)
        sc = sb("sc", [P, 12], F32)
        score_scale = {1: sc[:, 0:1], 2: sc[:, 1:2]}
        score_minus = {1: sc[:, 2:3], 2: sc[:, 3:4]}
        out_scale = {1: sc[:, 4:5], 2: sc[:, 5:6]}
        ff_scale = sc[:, 6:7]
        ff_up = sc[:, 7:8]
        part = sc[:, 8:12]

        ARENA = 85 * 256
        arena = sb("arena", [P, ARENA], F32)
        taken = [0]

        def carve(words):
            at = taken[0]
            taken[0] += words
            return arena[:, at:at + words]

        qkv = {}
        for s in range(SLOTS):
            qkv[s, "q"] = carve(AT * S).bitcast(F16).rearrange("p (i m n) -> p i m n", i=2, m=AT)
            qkv[s, "k"] = carve(AT * S).bitcast(F16).rearrange("p (i m n) -> p i m n", i=2, m=AT)
            qkv[s, "v"] = carve(TT * DA).bitcast(F16).rearrange("p (i t n) -> p i t n", i=2, t=TT)
        mixed = carve(AT * S).bitcast(F16).rearrange("p (i m n) -> p i m n", i=2, m=AT)
        probs = carve(2 * 2 * TT * S).rearrange("p (r h t k) -> p r h t k", r=2, h=2, t=TT)
        probsT = carve(4 * 512).bitcast(F16).rearrange("p (r i n) -> p r i n", r=4, i=2)
        gelu = carve(2 * S).rearrange("p (r n) -> p r n", r=2)
        gated = carve(2 * S).rearrange("p (r n) -> p r n", r=2)
        h32 = carve(KT * S).rearrange("p (k n) -> p k n", k=KT)
        hT = [carve(KT * S).bitcast(F16).rearrange("p (i k n) -> p i k n", i=2, k=KT) for _ in range(SLOTS)]
        c32 = carve(2 * SK).rearrange("p (k n) -> p k n", k=2)
        cT = [carve(2 * SK).bitcast(F16).rearrange("p (i k n) -> p i k n", i=2, k=2) for _ in range(SLOTS)]
        arena_words = taken[0]
        inner = [sb(f"inner_{i}", [P, 4, S], F32R) for i in ("high", "low")]

        xin = [sb(f"xin{s}", [P, TT, D], F32) for s in range(SLOTS)]
        xres = [sb(f"xres{s}", [P, TT, D], F32) for s in range(SLOTS)]
        xhat = [sb(f"xhat{s}", [P, TT, D], F32) for s in range(SLOTS)]
        stat6 = sb("stat6", [P, TT, 6], F32)
        moments = [sb(f"moments{s}", [P, TT, 2], F32) for s in range(SLOTS)]
        spread = [sb(f"spread{s}", [P, 2, TT], F32) for s in range(SLOTS)]
        cin = [sb(f"cin{s}", [P, DC], F32) for s in range(SLOTS)]
        peak = sb("peak", [P, 2, 4], F32)
        shift = sb("shift", [P, 2, 4], F32)
        total = sb("total", [P, 2, 4], F32)
        share = sb("share", [P, 2, 4], F32)

        score_ps = stack.enter_context(nc.psum_tensor("score_ps", [P, 2, 2, 512], F32))
        probsT_ps = stack.enter_context(nc.psum_tensor("probsT_ps", [P, 2, 512], F32))
        group_ps = stack.enter_context(nc.psum_tensor("group_ps", [P, 2, 512], F32))

        small_in = sem("small_in")
        staged = {n: sem(f"staged_{n}") for n in WEIGHTS + ["ff2", "ctx"]}
        const_ready = sem("const_ready")
        w2_ready = sem("w2_ready")
        setup = sem("setup")
        largest_ready = sem("largest_ready")
        vecs_turned = sem("vecs_turned")
        turned = sem("turned")
        diag_ready = sem("diag_ready")
        spread_out = sem("spread_out")
        scales_ready = sem("scales_ready")
        w_high = sem("w_high")
        w_ready = sem("w_ready")
        pool_past = sem("pool_past")
        dve_past = sem("dve_past")
        x_loaded = [sem(f"x_loaded{s}") for s in range(SLOTS)]
        c_loaded = [sem(f"c_loaded{s}") for s in range(SLOTS)]
        stored = [sem(f"stored{s}") for s in range(SLOTS)]
        stat_step = sem("stat_step")
        stats_ready = sem("stats_ready")
        root_step = sem("root_step")
        xhat_ready = sem("xhat_ready")
        x_biased = [sem(f"x_biased{s}") for s in range(SLOTS)]
        group_full = sem("group_full")
        group_done = sem("group_done")
        group_high = sem("group_high")
        h_high = sem("h_high")
        h_ready = sem("h_ready")
        c_high = sem("c_high")
        c_ready = sem("c_ready")
        scores_full = sem("scores_full")
        peak_ready = sem("peak_ready")
        shift_ready = sem("shift_ready")
        exp_done = sem("exp_done")
        share_ready = sem("share_ready")
        probs_ready = sem("probs_ready")
        probsT_full = sem("probsT_full")
        probsT_high = sem("probsT_high")
        probsT_ready = sem("probsT_ready")
        gelu_done = sem("gelu_done")
        gated_ready = sem("gated_ready")
        inner_high = sem("inner_high")
        inner_ready = sem("inner_ready")
        ff2_full = sem("ff2_full")
        result_ready = sem("result_ready")

        SMALL = 10
        x_view = x.rearrange("n (t p) d -> n p t d", p=P)
        out_view = out.rearrange("n (t p) d -> n p t d", p=P)

        stage, at = {}, 0
        for n in ["ff2", "wq1", "wk1", "wv1", "wo1", "wq2", "wk2", "wv2", "ff1"]:
            words = 16 * FF // 4 if n == "ff1" else 8 * DA // 4
            stage[n] = arena[:, at:at + words]
            at += words
        stage["wo2"] = stage["ff2"]
        assert max(at + 4 * DC, arena_words) <= ARENA
        view = {n: w[n].rearrange("(k p) n -> p k n", p=kp.get(n, P)) for n in WEIGHTS + ["ff2"]}
        LOADS = ["ff2", "wq1", "wk1", "wv1", "wo1", "wq2", "wk2", "wv2", "ff1", "wo2"]

        ctx_all = arena[:, at:at + 4 * DC].rearrange("p (n d) -> p n d", n=4)
        CCH = NB // 4
        ctx_max = sb("ctx_max", [P, CCH], F32)
        ctx_seen = sem("ctx_seen")

        def st(n):
            return stage[n].rearrange("p (k n) -> p k n", k=view[n].shape[1])

        def weight(n, i, k, a, z):
            return wsb[n][0:kp[n], i, k, a:z]

        THREE = ((0, 0), (0, 1), (1, 0))

        def proj_place(kind, s, j, bank, i):
            if kind in ("q1", "k1", "q2"):
                return qkv[s, kind[0]][:, i, 2 * j:2 * j + 2, :], bank.rearrange("p (m n) -> p m n", m=2), Q_SHIFT
            if kind == "v1":
                return qkv[s, "v"][:, i, j // 2, j % 2 * 512:j % 2 * 512 + 512], bank, Q_SHIFT
            if kind == "k2":
                return (qkv[s, "k"][:, i, 4 * j:4 * j + 4, 0:SK],
                        bank[:, 0:4 * SK].rearrange("p (m n) -> p m n", m=4), C_SHIFT)
            return qkv[s, "v"][0:SK, i, 0, j * 512:j * 512 + 512], bank[0:SK], C_SHIFT

        block = stack.enter_context(nc.Block())

        @block.sync
        def _(sp):
            for i in range(3):
                for c, v in enumerate((g[i], b[i])):
                    at = (2 * i + c) * KT
                    sp.dma_start(vec_rows[at:at + KT, :], v.rearrange("(k p) -> k p", p=P)).then_inc(small_in, 16)
                sp.dma_start(bias_rows[:, i, :], bo[i].partition_broadcast(P)).then_inc(small_in, 16)
            sp.dma_start(vec_rows[6 * KT:NVEC, :], b_ff1.rearrange("(m p) -> m p", p=P)).then_inc(small_in, 16)

            def load(turn):
                for s in range(SLOTS):
                    sp.dma_start(xin[s][:], x_view[turn * SLOTS + s]).then_inc(x_loaded[s], 16)
                    sp.dma_start(cin[s][0:SK, :], ctx[turn * SLOTS + s]).then_inc(c_loaded[s], 16)

            load(0)
            for s in range(SLOTS):
                sp.sem_inc(stored[s], 16)
            for n in LOADS:
                if n == "wo2":
                    sp.wait_ge(w2_ready, 2)
                sp.dma_start(st(n)[0:kp.get(n, P)], view[n]).then_inc(staged[n], 16)
                if n == "ff2":
                    for c in range(CCH):
                        if c:
                            sp.wait_ge(ctx_seen, c)
                        sp.dma_start(ctx_all[0:SK], ctx[4 * c:4 * c + 4].rearrange("n s d -> s n d")).then_inc(staged["ctx"], 16)

            def store(turn):
                for s in range(SLOTS):
                    sp.wait_ge(result_ready, turn * SLOTS + s + 1 + SLOTS)
                    sp.dma_start(out_view[turn * SLOTS + s], xres[s][:]).then_inc(stored[s], 16)

            with sp.Fori(0, TURNS_OF_LOOP - 1) as turn:
                for s in range(SLOTS):
                    sp.wait_ge(x_biased[s], turn * 3 + 1)
                    sp.dma_start(xin[s][:], x_view[turn * SLOTS + SLOTS + s]).then_inc(x_loaded[s], 16)
                for s in range(SLOTS):
                    sp.wait_ge(group_full, turn * NGROUP + GROUP["ctx", s] + 1)
                    sp.dma_start(cin[s][0:SK, :], ctx[turn * SLOTS + SLOTS + s]).then_inc(c_loaded[s], 16)
                store(turn)
            store(TURNS_OF_LOOP - 1)
            for s in range(SLOTS):
                sp.wait_ge(stored[s], 16 * TURNS_OF_LOOP + 16)

        @block.gpsimd
        def _(pool):
            nc.gpsimd.memset(ones[:], 1.0).then_inc(const_ready, 1)
            nc.gpsimd.memset(half[:], -0.5).then_inc(const_ready, 1)
            nc.gpsimd.memset(largest[:], 0.0).then_inc(const_ready, 1)
            nc.gpsimd.memset(ident[:], 0.0).then_inc(const_ready, 1)
            pool.wait_ge(const_ready, 4)
            nc.gpsimd.affine_select(out=ident[:], in_=ident[:], compare_op=ALU.not_equal, fill=1.0, base=0,
                                    pattern=[[-1, P]], channel_multiplier=1).then_inc(const_ready, 1)
            pool.wait_ge(const_ready, 5)
            pool.wait_ge(small_in, 16 * SMALL)

            def norm_rows(turn, s, n):
                i = STATS[s, n]
                pool.wait_ge(stats_ready, turn * NLN + i + 1 + 1)
                pool.sem_inc(pool_past, 1)
                nc.gpsimd.tensor_scalar(spread[s][:, 0, :], moments[s][:, :, 1], EPS, None, ALU.add).then_inc(root_step, 1)
                pool.wait_ge(root_step, turn * (2 * NLN) + 2 * i + 1)
                nc.gpsimd.tensor_tensor(spread[s][:, 1, :], spread[s][:, 0, :], half[:], ALU.pow).then_inc(root_step, 1)
                pool.wait_ge(root_step, turn * (2 * NLN) + 2 * i + 2)
                pool.sem_inc(pool_past, 1)
                rows = xin[s] if n == 1 else xres[s]
                for t in range(TT):
                    nc.gpsimd.tensor_scalar(xhat[s][:, t, :], rows[:, t, :], moments[s][:, t, 0:1], spread[s][:, 1, t:t + 1],
                                            ALU.subtract, ALU.mult).then_inc(xhat_ready, 1)
                pool.wait_ge(xhat_ready, turn * (TT * NLN) + TT * (i + 1))
                if n == 1:
                    pool.wait_ge(stored[s], turn * 16 + 16)
                ins = nc.gpsimd.tensor_tensor(xres[s][:], rows[:], bias_rows[:, n - 1:n, :].to_broadcast([P, TT, D]), ALU.add)
                ins.then_inc(x_biased[s], 1)

            def normalise(turn, p):
                _, a, _ = of_pair(p)
                K = S if a == 1 else SK
                pool.wait_ge(share_ready, turn * NPAIR + p + 1)
                pool.sem_inc(pool_past, 1)
                for h in range(2):
                    for t in range(TT):
                        rows = probs[:, p % 2, h, t, 0:K]
                        nc.gpsimd.tensor_scalar(rows, rows, share[:, p % 2, 2 * h + t:2 * h + t + 1], 2.0 ** BOUND,
                                                ALU.mult, ALU.mult).then_inc(probs_ready, 1)

            with pool.Fori(0, TURNS_OF_LOOP) as turn:
                for step in ORDER:
                    if step[0] == "stats":
                        norm_rows(turn, *step[1:])
                    elif step[0] == "norm":
                        normalise(turn, step[1])

        @block.scalar
        def _(act):
            act.wait_ge(scales_ready, 1)
            for n in WEIGHTS:
                act.wait_ge(staged[n], 16)
                nc.scalar.activation(wsb[n][0:kp[n], 0], st(n)[0:kp[n]], ACT.Copy, scale=up[0:kp[n], COL[n]:COL[n] + 1]).then_inc(w_high, 1)

            def group(turn, step):
                act.wait_ge(group_full, turn * NGROUP + GROUP[step] + 1)
                return group_ps[:, GROUP[step] % 2, :]

            def h_halves(turn, s, n):
                act.wait_ge(group_done, turn * NGROUP + GROUP["turn", s, n] + 1 + 2)
                nc.scalar.activation(hT[s][:, 0], h32[:], ACT.Copy).then_inc(h_high, 1)

            def c_halves(turn, s):
                act.wait_ge(group_done, turn * NGROUP + GROUP["ctx", s] + 1 + 2)
                nc.scalar.activation(cT[s][0:KC, 0], c32[0:KC], ACT.Copy).then_inc(c_high, 1)

            def proj(turn, step):
                _, s, kind, j = step
                bank = group(turn, step)
                dst, src, shift_bits = proj_place(kind, s, j, bank, 0)
                nc.scalar.activation(dst, src, ACT.Copy, scale=2.0 ** -shift_bits).then_inc(group_high, 1)

            def exponentials(turn, p):
                _, a, _ = of_pair(p)
                K = S if a == 1 else SK
                act.wait_ge(shift_ready, turn * NPAIR + p + 1)
                if p >= 2:
                    act.wait_ge(probsT_full, turn * NUNIT + units(p - 2)[-1] + 1)
                for h in range(2):
                    for t in range(TT):
                        i = 2 * h + t
                        ins = nc.scalar.activation(probs[:, p % 2, h, t, 0:K], score_ps[:, p % 2, h, t * K:t * K + K], ACT.Exp,
                                                   scale=score_scale[a], bias=shift[:, p % 2, i:i + 1],
                                                   accum_out=total[:, p % 2, i:i + 1])
                ins.then_inc(exp_done, 1)

            def probs_high(turn, p):
                K = S if p < 2 * PAIRS else SK
                R = P if p < 2 * PAIRS else SK
                for u in units(p):
                    act.wait_ge(probsT_full, turn * NUNIT + u + 1)
                    nc.scalar.activation(probsT[0:R, u % 4, 0, :], probsT_ps[0:R, u % 2, :], ACT.Copy).then_inc(probsT_high, 1)

            def mix(turn, step):
                _, _, j = of_pair(step[1])
                bank = group(turn, step)
                nc.scalar.activation(mixed[:, 0, j, :], bank[:, 0:S], ACT.Copy, scale=2.0 ** -BOUND).then_inc(group_high, 1)

            def gate(turn, step):
                _, s, j = step
                bank = group(turn, step)
                nc.scalar.activation(gelu[:, j % 2, :], bank[:, S:2 * S], ACT.Gelu, scale=ff_scale,
                                     bias=ffb[:, FT + j:FT + j + 1]).then_inc(gelu_done, 1)

            with act.Fori(0, TURNS_OF_LOOP) as turn:
                for step in ORDER:
                    if step[0] == "turn":
                        h_halves(turn, *step[1:])
                    elif step[0] == "ctx":
                        c_halves(turn, step[1])
                    elif step[0] == "proj":
                        proj(turn, step)
                    elif step[0] == "exp":
                        exponentials(turn, step[1])
                    elif step[0] == "split_probs":
                        probs_high(turn, step[1])
                    elif step[0] == "mix":
                        mix(turn, step)
                    elif step[0] == "ff1":
                        gate(turn, step)

        @block.vector
        def _(dve):
            count = [0]

            def link(ins):
                count[0] += 1
                ins.then_inc(setup, 1)
                dve.wait_ge(setup, count[0])

            dve.wait_ge(staged["ff2"], 16)
            nc.vector.tensor_copy(w2sb[0][:], st("ff2")).then_inc(w2_ready, 1)
            dve.wait_ge(w2_ready, 1)
            nc.vector.tensor_tensor(w2sb[1][:], st("ff2"), w2sb[0][:].bitcast(F32), ALU.subtract).then_inc(w2_ready, 1)
            dve.wait_ge(w2_ready, 2)
            dve.wait_ge(const_ready, 5)
            for c in range(CCH):
                dve.wait_ge(staged["ctx"], 16 * (c + 1))
                nc.vector.tensor_reduce(ctx_max[0:SK, c:c + 1], ctx_all[0:SK], AX.XY, ALU.max, apply_absolute_value=True).then_inc(ctx_seen, 1)
            dve.wait_ge(ctx_seen, CCH)
            link(nc.vector.tensor_reduce(largest[0:SK, COL["ctx"]:COL["ctx"] + 1], ctx_max[0:SK], AX.X, ALU.max))
            dve.wait_ge(vecs_turned, 1)
            link(nc.vector.tensor_copy(vecs[:], group_ps[:, 1, 0:NVEC]))
            for i in range(3):
                for c, n in enumerate(("h", "b")):
                    k = COL[f"{n}{i + 1}"]
                    link(nc.vector.tensor_reduce(largest[:, k:k + 1], gains[:, i, c, :], AX.X, ALU.max, apply_absolute_value=True))
            for n in WEIGHTS:
                dve.wait_ge(staged[n], 16)
                link(nc.vector.tensor_reduce(largest[0:kp[n], COL[n]:COL[n] + 1], st(n)[0:kp[n]], AX.XY, ALU.max, apply_absolute_value=True))
            dve.sem_inc(largest_ready, 1)
            dve.wait_ge(turned, 1)
            link(nc.vector.tensor_reduce(top[:], group_ps[0:NCOL, 0, 0:P], AX.X, ALU.max))
            nc.vector.tensor_scalar(diag[:], ident[0:NCOL, 0:NCOL], top[:, 0:1], None, ALU.mult).then_inc(diag_ready, 1)
            dve.wait_ge(spread_out, 1)
            link(nc.vector.tensor_copy(bound[:], group_ps[:, 1, 0:NCOL]))
            h, hb = COL["h1"], COL["b1"]
            link(nc.vector.tensor_tensor(bound[:, h:h + 3], bound[:, h:h + 3], bound[:, hb:hb + 3], ALU.add))
            link(nc.vector.tensor_scalar(bound[:, h:h + 3], bound[:, h:h + 3], float(D) ** 0.5, None, ALU.mult))
            link(nc.vector.tensor_scalar(bound[:], bound[:], FLOOR, None, ALU.max))
            link(nc.vector.tensor_scalar(power[:].bitcast(I32), bound[:].bitcast(I32), EXPONENT, None, ALU.bitwise_and))
            link(nc.vector.reciprocal(up[:], power[:]))
            link(nc.vector.tensor_scalar(up[:], up[:], 2.0 ** (BOUND - 1), None, ALU.mult))
            link(nc.vector.tensor_scalar(down[:], power[:], 2.0 ** (1 - BOUND), None, ALU.mult))

            def times(dst, one, two, factor):
                link(nc.vector.scalar_tensor_tensor(dst, one, factor, two, ALU.mult, ALU.mult))

            def d(n):
                return down[:, COL[n]:COL[n] + 1]

            def u(n):
                return up[:, COL[n]:COL[n] + 1]

            times(part[:, 0:1], d("h1"), d("wq1"), 2.0 ** Q_SHIFT)
            times(part[:, 1:2], d("h1"), d("wk1"), 2.0 ** Q_SHIFT)
            times(score_scale[1], part[:, 0:1], part[:, 1:2], SCALE)
            times(part[:, 2:3], d("h2"), d("wq2"), 2.0 ** Q_SHIFT)
            times(part[:, 3:4], d("ctx"), d("wk2"), 2.0 ** C_SHIFT)
            times(score_scale[2], part[:, 2:3], part[:, 3:4], SCALE)
            for a in (1, 2):
                link(nc.vector.tensor_scalar(score_minus[a], score_scale[a], -1.0, None, ALU.mult))
            times(part[:, 0:1], d("h1"), d("wv1"), 2.0 ** Q_SHIFT)
            times(out_scale[1], part[:, 0:1], d("wo1"), 1.0)
            times(part[:, 1:2], d("ctx"), d("wv2"), 2.0 ** C_SHIFT)
            times(out_scale[2], part[:, 1:2], d("wo2"), 1.0)
            times(ff_scale, d("h3"), d("ff1"), 1.0)
            times(ff_up, u("h3"), u("ff1"), 1.0)
            link(nc.vector.tensor_scalar(ffb_a[:], ffb[:, 0:FT], ff_up, None, ALU.mult))
            for i in range(3):
                link(nc.vector.tensor_scalar(gains_s[:, i], gains[:, i], u(f"h{i + 1}"), None, ALU.mult))
            dve.sem_inc(scales_ready, 1)
            for i, n in enumerate(WEIGHTS):
                dve.wait_ge(w_high, i + 1)
                nc.vector.scalar_tensor_tensor(wsb[n][0:kp[n], 1], st(n)[0:kp[n]], up[0:kp[n], COL[n]:COL[n] + 1], wsb[n][0:kp[n], 0],
                                               ALU.mult, ALU.subtract).then_inc(w_ready, 1)
            dve.sem_inc(group_done, 2)
            dve.sem_inc(probsT_ready, 2)
            dve.sem_inc(result_ready, SLOTS)
            dve.sem_inc(stats_ready, 1)

            def group(turn, step):
                dve.wait_ge(group_full, turn * NGROUP + GROUP[step] + 1)
                return group_ps[:, GROUP[step] % 2, :]

            def stats(turn, s, n):
                i = STATS[s, n]
                if n == 1:
                    dve.wait_ge(x_loaded[s], turn * 16 + 16)
                else:
                    dve.wait_ge(group_done, turn * NGROUP + GROUP["out", s, n - 1, TT - 1] + 1 + 2)
                rows = xin[s] if n == 1 else xres[s]
                dve.wait_ge(stats_ready, turn * NLN + i + 1)
                for t in range(TT):
                    ins = nc.vector.bn_stats(stat6[:, t, :], rows[:, t, :])
                ins.then_inc(stat_step, 1)
                dve.wait_ge(stat_step, turn * NLN + i + 1)
                dve.sem_inc(dve_past, 1)
                for t in range(TT):
                    ins = nc.vector.bn_aggr(moments[s][:, t, :], stat6[:, t, :])
                ins.then_inc(stats_ready, 1)

            def h_halves(turn, step):
                _, s, n = step
                i = TURNS[s, n]
                bank = group(turn, step)
                for k in range(KT):
                    ins = nc.vector.tensor_scalar(h32[:, k, :], bank[:, k * S:k * S + S], gains_s[:, n - 1, 0, k:k + 1],
                                                  gains_s[:, n - 1, 1, k:k + 1], ALU.mult, ALU.add)
                ins.then_inc(group_done, 1)
                dve.wait_ge(h_high, turn * NLN + i + 1)
                nc.vector.tensor_tensor(hT[s][:, 1], h32[:], hT[s][:, 0], ALU.subtract).then_inc(h_ready, 1)

            def c_halves(turn, step):
                _, s = step
                bank = group(turn, step)
                nc.vector.tensor_scalar(c32[0:KC], bank[0:KC, 0:2 * SK].rearrange("p (k n) -> p k n", k=2), u("ctx")[0:KC], None,
                                        ALU.mult).then_inc(group_done, 1)
                dve.wait_ge(c_high, turn * SLOTS + CTXS[s] + 1)
                nc.vector.tensor_tensor(cT[s][0:KC, 1], c32[0:KC], cT[s][0:KC, 0], ALU.subtract).then_inc(c_ready, 1)

            def low(turn, step, dst, src, high, factor):
                dve.wait_ge(group_high, turn * NHIGH + HIGH[step] + 1)
                nc.vector.scalar_tensor_tensor(dst, src, factor, high, ALU.mult, ALU.subtract).then_inc(group_done, 1)

            def proj(turn, step):
                _, s, kind, j = step
                bank = group_ps[:, GROUP[step] % 2, :]
                high, src, shift_bits = proj_place(kind, s, j, bank, 0)
                dst, _, _ = proj_place(kind, s, j, bank, 1)
                low(turn, step, dst, src, high, 2.0 ** -shift_bits)

            def mix(turn, step):
                _, _, j = of_pair(step[1])
                low(turn, step, mixed[:, 1, j, :], group_ps[:, GROUP[step] % 2, 0:S], mixed[:, 0, j, :], 2.0 ** -BOUND)

            def maxima(turn, p):
                _, a, _ = of_pair(p)
                K = S if a == 1 else SK
                dve.wait_ge(scores_full, turn * NPAIR + p + 1)
                nc.vector.tensor_reduce(peak[:, p % 2, :].rearrange("p (h t) -> p h t", h=2),
                                        score_ps[:, p % 2, :, 0:TT * K].rearrange("p h (t k) -> p h t k", t=TT),
                                        AX.X, ALU.max).then_inc(peak_ready, 1)
                dve.wait_ge(peak_ready, turn * NPAIR + p + 1)
                nc.vector.tensor_scalar(shift[:, p % 2, :], peak[:, p % 2, :], score_minus[a], None, ALU.mult).then_inc(shift_ready, 1)

            def shares(turn, p):
                dve.wait_ge(exp_done, turn * NPAIR + p + 1)
                nc.vector.reciprocal(share[:, p % 2, :], total[:, p % 2, :]).then_inc(share_ready, 1)

            def probs_low(turn, p):
                R = P if p < 2 * PAIRS else SK
                for unit in units(p):
                    dve.wait_ge(probsT_high, turn * NUNIT + unit + 1)
                    nc.vector.tensor_tensor(probsT[0:R, unit % 4, 1, :], probsT_ps[0:R, unit % 2, :], probsT[0:R, unit % 4, 0, :],
                                            ALU.subtract).then_inc(probsT_ready, 1)

            def residual(turn, step):
                _, s, n, t = step
                bank = group(turn, step)
                dve.wait_ge(x_biased[s], turn * 3 + n)
                nc.vector.scalar_tensor_tensor(xres[s][:, t, :], bank[:, 0:D], out_scale[n], xres[s][:, t, :],
                                               ALU.mult, ALU.add).then_inc(group_done, 1)

            def inner_halves(turn, step):
                _, s, j = step
                i = TILES[s, j]
                dve.wait_ge(gelu_done, turn * NTILE + i + 1)
                bank = group_ps[:, GROUP[step] % 2, :]
                nc.vector.scalar_tensor_tensor(gated[:, j % 2, :], bank[:, 0:S], ffb_a[:, j:j + 1], gelu[:, j % 2, :],
                                               ALU.add, ALU.mult).then_inc(group_done, 1)
                dve.wait_ge(group_done, turn * NGROUP + GROUP[step] + 1 + 2)
                nc.vector.tensor_copy(inner[0][:, j % 4, :], gated[:, j % 2, :]).then_inc(inner_high, 1)
                dve.wait_ge(inner_high, turn * NTILE + i + 1)
                nc.vector.tensor_tensor(inner[1][:, j % 4, :], gated[:, j % 2, :], inner[0][:, j % 4, :].bitcast(F32),
                                        ALU.subtract).then_inc(inner_ready, 1)

            def finish(turn, s):
                dve.wait_ge(ff2_full, turn * SLOTS + s + 1)
                dve.wait_ge(x_biased[s], turn * 3 + 3)
                ins = nc.vector.scalar_tensor_tensor(xres[s][:], score_ps[:, s, :, 0:D], ff_scale, xres[s][:], ALU.mult, ALU.add)
                ins.then_inc(result_ready, 1)

            with dve.Fori(0, TURNS_OF_LOOP) as turn:
                for step in ORDER:
                    if step[0] == "stats":
                        stats(turn, *step[1:])
                    elif step[0] == "turn":
                        h_halves(turn, step)
                    elif step[0] == "ctx":
                        c_halves(turn, step)
                    elif step[0] == "proj":
                        proj(turn, step)
                    elif step[0] == "scores":
                        maxima(turn, step[1])
                    elif step[0] == "norm":
                        shares(turn, step[1])
                    elif step[0] == "split_probs":
                        probs_low(turn, step[1])
                    elif step[0] == "mix":
                        mix(turn, step)
                    elif step[0] == "out":
                        residual(turn, step)
                    elif step[0] == "ff1":
                        inner_halves(turn, step)
                    elif step[0] == "finish":
                        finish(turn, step[1])

        @block.tensor
        def _(pe):
            pe.wait_ge(const_ready, 5)
            pe.wait_ge(small_in, 16 * SMALL)
            nc.tensor.transpose(group_ps[:, 1, 0:NVEC], vec_rows[:], ident[0:NVEC, 0:NVEC]).then_inc(vecs_turned, 1)
            pe.wait_ge(largest_ready, 1)
            nc.tensor.transpose(group_ps[0:NCOL, 0, 0:P], largest[:], ident[:]).then_inc(turned, 1)
            pe.wait_ge(diag_ready, 1)
            nc.tensor.matmul(group_ps[:, 1, 0:NCOL], ones[:], diag[:], start=True, stop=True).then_inc(spread_out, 1)
            pe.wait_ge(w_ready, len(WEIGHTS))

            def group(turn, step):
                pe.wait_ge(group_done, turn * NGROUP + GROUP[step] + 1)
                return group_ps[:, GROUP[step] % 2, :]

            def done(turn, step):
                pe.wait_ge(group_done, turn * NGROUP + GROUP[step] + 1 + 2)

            def turn_rows(turn, step):
                _, s, n = step
                pe.wait_ge(xhat_ready, turn * (TT * NLN) + TT * (STATS[s, n] + 1))
                bank = group(turn, step)
                for k in range(KT):
                    for t in range(TT):
                        ins = nc.tensor.transpose(bank[:, k * S + t * P:k * S + t * P + P], xhat[s][:, t, k * P:k * P + P], ident[:])
                ins.then_inc(group_full, 1)

            def turn_ctx(turn, step):
                _, s = step
                pe.wait_ge(c_loaded[s], turn * 16 + 16)
                bank = group(turn, step)
                for k in range(2):
                    ins = nc.tensor.transpose(bank[0:KC, k * SK:k * SK + SK], cin[s][0:SK, k * KC:k * KC + KC], ident[0:SK, 0:SK])
                ins.then_inc(group_full, 1)

            def proj(turn, step):
                _, s, kind, j = step
                if kind[1] == "1":
                    pe.wait_ge(h_ready, turn * NLN + TURNS[s, 1] + 1)
                elif kind == "q2":
                    pe.wait_ge(h_ready, turn * NLN + TURNS[s, 2] + 1)
                else:
                    pe.wait_ge(c_ready, turn * SLOTS + CTXS[s] + 1)
                bank = group(turn, step)
                name = "w" + kind
                if kind in ("q1", "k1", "q2", "k2"):
                    src = cT[s][0:KC] if kind == "k2" else hT[s]
                    n, per = (SK, 4) if kind == "k2" else (S, 2)
                    for m in range(per):
                        mt = per * j + m
                        for k in range(2):
                            for i, (a, z) in enumerate(THREE):
                                ins = nc.tensor.matmul(bank[:, m * n:m * n + n], weight(name, z, k, mt * P, mt * P + P), src[:, a, k, :],
                                                       start=(k == 0 and i == 0), stop=(k == 1 and i == 2))
                else:
                    t, c = (j // 2, j % 2) if kind == "v1" else (0, j)
                    M = P if kind == "v1" else SK
                    src = hT[s] if kind == "v1" else cT[s][0:KC]
                    for k in range(2):
                        for i, (a, z) in enumerate(THREE):
                            ins = nc.tensor.matmul(bank[0:M], src[:, a, k, t * P:t * P + M], weight(name, z, k, c * 512, c * 512 + 512),
                                                   start=(k == 0 and i == 0), stop=(k == 1 and i == 2))
                ins.then_inc(group_full, 1)

            def scores(turn, p):
                s, a, j = of_pair(p)
                done(turn, ("proj", s, f"q{a}", j // 2))
                done(turn, ("proj", s, f"k{a}", j // 2 if a == 1 else j // 4))
                if p < 2:
                    pe.wait_ge(result_ready, turn * SLOTS + p + 1)
                else:
                    pe.wait_ge(exp_done, turn * NPAIR + p - 1)
                K = S if a == 1 else SK
                q, k = qkv[s, "q"], qkv[s, "k"]
                for t in range(TT):
                    for i, (a_, z) in enumerate(THREE):
                        for h in range(2):
                            r = slice(h * DH, h * DH + DH)
                            ins = nc.tensor.matmul(score_ps[:, p % 2, h, t * K:t * K + K], q[r, a_, j, t * P:t * P + P], k[r, z, j, 0:K],
                                                   start=(i == 0), stop=(i == 2))
                ins.then_inc(scores_full, 1)

            def turn_probs(turn, p):
                _, a, _ = of_pair(p)
                pe.wait_ge(probs_ready, turn * (4 * NPAIR) + 4 * (p + 1))
                for h in range(2):
                    u = units(p)[h if a == 1 else 0]
                    if a == 1 or h == 0:
                        pe.wait_ge(probsT_ready, turn * NUNIT + u + 1)
                    for k in range(TT if a == 1 else 1):
                        K = P if a == 1 else SK
                        for t in range(TT):
                            at = (k if a == 1 else h) * S + t * P
                            ins = nc.tensor.transpose(probsT_ps[0:K, u % 2, at:at + P], probs[:, p % 2, h, t, k * P:k * P + K], ident[:])
                    if a == 1 or h == 1:
                        ins.then_inc(probsT_full, 1)

            def mix(turn, step):
                p = step[1]
                s, a, j = of_pair(p)
                if a == 1:
                    done(turn, ("proj", s, "v1", 2 + j // 4))
                else:
                    done(turn, ("proj", s, "v2", j // 4))
                pe.wait_ge(probsT_ready, turn * NUNIT + units(p)[-1] + 1 + 2)
                bank = group(turn, step)
                v = qkv[s, "v"]
                kts = TT if a == 1 else 1
                K = P if a == 1 else SK
                for k in range(kts):
                    for i, (a_, z) in enumerate(THREE):
                        for h in range(2):
                            u = units(p)[h if a == 1 else 0]
                            at = (k if a == 1 else h) * S
                            ins = nc.tensor.matmul(bank[h * DH:h * DH + DH, 0:S], v[0:K, z, k, (2 * j + h) * DH:(2 * j + h + 1) * DH],
                                                   probsT[0:K, u % 4, a_, at:at + S], start=(k == 0 and i == 0), stop=(k == kts - 1 and i == 2))
                ins.then_inc(group_full, 1)

            def project_out(turn, step):
                _, s, n, t = step
                last = (n - 1) * 2 * PAIRS + s * PAIRS + PAIRS - 1
                done(turn, ("mix", last))
                bank = group(turn, step)
                for c in range(AT):
                    for i, (a, z) in enumerate(THREE):
                        ins = nc.tensor.matmul(bank[:, 0:D], mixed[:, a, c, t * P:t * P + P], wsb[f"wo{n}"][:, z, c, :],
                                               start=(c == 0 and i == 0), stop=(c == AT - 1 and i == 2))
                ins.then_inc(group_full, 1)

            def ff1(turn, step):
                _, s, j = step
                pe.wait_ge(h_ready, turn * NLN + TURNS[s, 3] + 1)
                bank = group(turn, step)
                for half_ in (1, 0):
                    at = half_ * FF + j * P
                    for k in range(KT):
                        for i, (a, z) in enumerate(THREE):
                            ins = nc.tensor.matmul(bank[:, half_ * S:half_ * S + S], weight("ff1", z, k, at, at + P), hT[s][:, a, k, :],
                                                   start=(k == 0 and i == 0), stop=(k == KT - 1 and i == 2))
                ins.then_inc(group_full, 1)

            def ff2(turn, step):
                _, s, j = step
                if j == 0:
                    pe.wait_ge(exp_done, turn * NPAIR + NPAIR - 1 + s)
                pe.wait_ge(inner_ready, turn * NTILE + TILES[s, j] + 1)
                for t in range(TT):
                    for i, (a, z) in enumerate(THREE):
                        ins = nc.tensor.matmul(score_ps[:, s, t, 0:D], inner[a][:, j % 4, t * P:t * P + P], w2sb[z][:, j, :],
                                               start=(j == 0 and i == 0), stop=(j == FT - 1 and i == 2))
                if j == FT - 1:
                    ins.then_inc(ff2_full, 1)

            with pe.Fori(0, TURNS_OF_LOOP) as turn:
                for step in ORDER:
                    if step[0] == "turn":
                        turn_rows(turn, step)
                    elif step[0] == "ctx":
                        turn_ctx(turn, step)
                    elif step[0] == "proj":
                        proj(turn, step)
                    elif step[0] == "scores":
                        scores(turn, step[1])
                    elif step[0] == "turn_probs":
                        turn_probs(turn, step[1])
                    elif step[0] == "mix":
                        mix(turn, step)
                    elif step[0] == "out":
                        project_out(turn, step)
                    elif step[0] == "ff1":
                        ff1(turn, step)
                    elif step[0] == "ff2":
                        ff2(turn, step)


def kernel(**inputs):
    import numpy as np
    import concourse.bacc as bacc
    from concourse.bass_utils import run_bass_kernel_spmd

    nc = bacc.Bacc("TRN2", target_bir_lowering=False, num_devices=1, dynamic_dma_scratch_size=2048)
    arrays, aps = {}, {}
    for name, value in inputs.items():
        array = np.ascontiguousarray(value)
        arrays[f"in_{name}"] = array
        aps[name] = nc.dram_tensor(f"in_{name}", array.shape, mybir.dt.from_np(array.dtype), kind="ExternalInput").ap()
    shape = inputs["x"].shape
    out = nc.dram_tensor("out", shape, F32, kind="ExternalOutput").ap()

    def of(name):
        return aps["L0_xattn_" + name]

    w = {n: of(n) for n in WEIGHTS if n != "ff1"}
    w["ff1"], w["ff2"] = of("w_ff1"), of("w_ff2")
    bass_xattn_block(nc, aps["x"], aps["ctx_768"], w, [of(f"g{i}") for i in (1, 2, 3)], [of(f"b{i}") for i in (1, 2, 3)],
                     [of("bo1"), of("bo2"), of("b_ff2")], of("b_ff1"), out)
    result = run_bass_kernel_spmd(nc, [arrays], core_ids=[0])
    return result.results[0]["out"]
```

```python
from contextlib import ExitStack

import concourse.bass as bass
from concourse import mybir

ALU = mybir.AluOpType
ACT = mybir.ActivationFunctionType
AX = mybir.AxisListType
F32, F16, F32R, I32 = mybir.dt.float32, mybir.dt.float16, mybir.dt.float32r, mybir.dt.int32

P = 128
HEADS, DH = 16, 64
PAIRS = HEADS // 2
EPS = 1e-5
SLOTS = 2

BOUND = 14
Q_SHIFT = 18
C_SHIFT = 22
FLOOR = 2.0 ** -20
EXPONENT = 0x7F800000

WEIGHTS = ["wq1", "wk1", "wv1", "wo1", "wq2", "wk2", "wv2", "wo2", "ff1"]
COL = {n: i for i, n in enumerate(WEIGHTS + ["ctx", "h1", "h2", "h3", "b1", "b2", "b3"])}
NCOL = 16


A, B = range(SLOTS)


def make_order():
    def proj(s, *names):
        return [("proj", s, n[:2], int(n[2])) for n in names]

    def out(s, n):
        return [("out", s, n, 0), ("out", s, n, 1), ("stats", s, n + 1)]

    def ff1(*tiles):
        return [("ff1", A, j) for j in tiles]

    order = proj(A, "q10", "k10") + [("scores", 0), ("exp", 0), ("scores", 1), ("exp", 1)]
    order += proj(A, "q11", "k11", "v10", "v12") + [("bias", A), ("bias", B)]
    fills = {
        0: proj(A, "q12", "k12"), 1: proj(A, "q13", "k13"), 2: proj(A, "v11", "v13"),
        3: proj(B, "q10", "k10"), 4: proj(B, "q11", "k11"), 5: proj(B, "v10", "v12"), 6: proj(B, "q12"),
        7: proj(B, "k12", "q13"), 8: proj(B, "k13"), 9: out(A, 1), 10: [("rows", A, 2)] + proj(B, "v11", "v13"),
        11: [("ctx", A), ("turn", A, 2)] + proj(A, "k20"), 12: proj(A, "q20", "v20"), 13: proj(A, "q21"),
        14: proj(A, "k21", "q22"), 15: proj(A, "v21", "q23"), 16: [("ctx", B)] + proj(B, "k20"),
        17: out(B, 1), 18: [("rows", B, 2)] + proj(B, "v20"), 19: [("turn", B, 2)] + proj(B, "q20"), 20: proj(B, "q21"),
        21: proj(B, "k21"), 22: proj(B, "q22"), 23: proj(B, "q23"), 24: proj(B, "v21"),
        25: out(A, 2), 26: [("rows", A, 3)], 27: [("turn", A, 3)] + ff1(0), 28: ff1(1, 2), 29: ff1(3), 30: ff1(4, 5), 31: ff1(6, 7),
    }
    last = 4 * PAIRS - 1
    order.append(("norm", 0))
    for p in range(last + 1):
        fill = list(fills.get(p, []))
        if p + 1 <= last:
            order.append(("norm", p + 1))
        if p + 2 <= last:
            order.append(("scores", p + 2))
            order += fill[:1]
            order.append(("exp", p + 2))
            order += fill[1:]
        else:
            order += fill
        order += [("turn_probs", p), ("split_probs", p)]
        if p >= 1:
            order.append(("mix", p - 1))
    order.append(("mix", last))

    def gates(s, i):
        return [("gate", s, 2 * i), ("gate", s, 2 * i + 1)]

    order += gates(A, 0) + [("out", B, 2, 0)] + gates(A, 1) + [("inner", A, 0), ("out", B, 2, 1), ("stats", B, 3)]
    order += [("ff2", A, 0), ("ff2", A, 1)] + gates(A, 2) + [("inner", A, 1), ("rows", B, 3), ("ff2", A, 2), ("ff2", A, 3)]
    order += [("turn", B, 3)] + gates(A, 3) + [("inner", A, 2), ("inner", A, 3)]
    order += [("ff1", B, 0), ("ff2", A, 4), ("ff1", B, 1), ("ff2", A, 5)] + gates(B, 0)
    order += [("ff1", B, 2), ("ff2", A, 6), ("ff1", B, 3), ("ff2", A, 7), ("finish", A)] + gates(B, 1) + [("inner", B, 0)]
    order += [("stats", A, 1), ("stats", B, 1)]
    order += [("ff1", B, 4), ("ff1", B, 5), ("ff2", B, 0), ("ff2", B, 1)] + gates(B, 2) + [("inner", B, 1)]
    order += [("rows", A, 1), ("rows", B, 1)]
    order += [("ff1", B, 6), ("ff1", B, 7), ("ff2", B, 2), ("ff2", B, 3)] + gates(B, 3) + [("inner", B, 2), ("turn", A, 1), ("turn", B, 1)]
    order += [("inner", B, 3), ("ff2", B, 4), ("ff2", B, 5), ("ff2", B, 6), ("ff2", B, 7), ("finish", B)]
    return order


BEFORE = [(x, s, 1) for x in ("stats", "rows", "turn") for s in range(SLOTS)]
ORDER = make_order()
RING = 4


def units(p):
    return [2 * p, 2 * p + 1] if p < 2 * PAIRS else [2 * PAIRS + p]


def groups_of(steps):
    taken = []
    for step in steps:
        if step[0] == "turn_probs":
            taken += [("probs", u) for u in units(step[1])]
        elif step[0] in ("turn", "proj", "ctx", "mix", "out", "ff1"):
            taken.append(step)
    return {step: i for i, step in enumerate(taken)}


def places(*kinds):
    return {step: i for i, step in enumerate(x for x in ORDER if x[0] in kinds)}


GROUP, GROUP_BEFORE = groups_of(ORDER), groups_of(BEFORE)
NGROUP = len(GROUP)
HIGH = places("proj", "mix")
NHIGH = len(HIGH)
LN = {step[1:]: i for step, i in places("stats").items()}
LN_BEFORE = {(s, 1): s for s in range(SLOTS)}
CTXS = {step[1]: i for step, i in places("ctx").items()}
NPAIR = 4 * PAIRS
NUNIT = units(NPAIR - 1)[-1] + 1
NLN = len(LN)
NTILE = 8 * SLOTS
assert NGROUP % RING == 0 and NPAIR % 4 == 0 and NUNIT % 4 == 0
assert all([x[1:] for x in ORDER if x[0] == kind] == list(LN) for kind in ("rows", "turn"))
assert [LN[s, 1] for s in range(SLOTS)] == [NLN - 2, NLN - 1]


def group_of(turn, step):
    return GROUP_BEFORE[step] if turn is None else turn * NGROUP + len(GROUP_BEFORE) + GROUP[step]


def bank_of(turn, step):
    return (GROUP_BEFORE[step] if turn is None else len(GROUP_BEFORE) + GROUP[step]) % RING


def ln_of(turn, s, n):
    return LN_BEFORE[s, n] if turn is None else turn * NLN + len(LN_BEFORE) + LN[s, n]


def of_pair(p):
    return p // PAIRS % 2, p // (2 * PAIRS) + 1, p % PAIRS


def bass_xattn_block(nc, x, ctx, w, g, b, bo, b_ff1, out):
    NB, S, D = x.shape
    SK, DC = ctx.shape[1], ctx.shape[2]
    DA = HEADS * DH
    FF = w["ff2"].shape[0]
    KT, TT, AT = D // P, S // P, DA // P
    FT = FF // P
    KC = DC // 2
    TURNS_OF_LOOP = NB // SLOTS
    SCALE = DH ** -0.5
    assert D == 256 and S == 256 and SK <= P and KC <= P and AT == PAIRS and FT == 8

    with ExitStack() as stack:
        def sb(name, shape, dt):
            return stack.enter_context(nc.sbuf_tensor(name, shape, dt))

        def sem(name):
            return stack.enter_context(nc.semaphore(name))

        kp = {n: KC if n in ("wk2", "wv2") else P for n in WEIGHTS}
        shape = {n: [2, AT, D] if n in ("wo1", "wo2") else [2, 2, 2 * FF] if n == "ff1" else [2, 2, DA] for n in WEIGHTS}
        wsb = {n: sb(n, [P] + shape[n], F16) for n in WEIGHTS}
        w2sb = [sb(f"w2_{i}", [P, FT, D], F32R) for i in ("high", "low")]
        ident = sb("ident", [P, P], F32)
        ones = sb("ones", [NCOL, P], F32)
        half = sb("half", [P, TT], F32)
        bias_rows = sb("bias_rows", [P, 3, D], F32)
        NVEC = 3 * 2 * KT + 2 * FT
        vec_rows = sb("vec_rows", [NVEC, P], F32)
        vecs = sb("vecs", [P, NVEC], F32)
        gains = vecs[:, 0:6 * KT].rearrange("p (i c k) -> p i c k", i=3, c=2)
        ffb = vecs[:, 6 * KT:NVEC]
        gains_s = sb("gains_s", [P, 3, 2, KT], F32)
        ffb_a = sb("ffb_a", [P, FT], F32)
        largest = sb("largest", [P, NCOL], F32)
        top = sb("top", [NCOL, 1], F32)
        diag = sb("diag", [NCOL, NCOL], F32)
        bound = sb("bound", [P, NCOL], F32)
        power = sb("power", [P, NCOL], F32)
        up = sb("up", [P, NCOL], F32)
        down = sb("down", [P, NCOL], F32)
        sc = sb("sc", [P, 12], F32)
        score_scale = {1: sc[:, 0:1], 2: sc[:, 1:2]}
        score_minus = {1: sc[:, 2:3], 2: sc[:, 3:4]}
        out_scale = {1: sc[:, 4:5], 2: sc[:, 5:6]}
        ff_scale = sc[:, 6:7]
        ff_up = sc[:, 7:8]
        part = sc[:, 8:12]

        ARENA = 97 * 256
        arena = sb("arena", [P, ARENA], F32)
        taken = [0]

        def carve(words):
            at = taken[0]
            taken[0] += words
            return arena[:, at:at + words]

        qkv = {}
        raw = arena[:, 0:2 * AT * S].rearrange("p (j n) -> p j n", j=FT)
        for s in range(SLOTS):
            qkv[s, "q"] = carve(AT * S).bitcast(F16).rearrange("p (i m n) -> p i m n", i=2, m=AT)
            qkv[s, "k"] = carve(AT * S).bitcast(F16).rearrange("p (i m n) -> p i m n", i=2, m=AT)
            qkv[s, "v"] = carve(TT * DA).bitcast(F16).rearrange("p (i t n) -> p i t n", i=2, t=TT)
        mixed = carve(AT * S).bitcast(F16).rearrange("p (i m n) -> p i m n", i=2, m=AT)
        probs = carve(4 * 2 * TT * S).rearrange("p (r h t k) -> p r h t k", r=4, h=2, t=TT)
        probsT = carve(4 * 512).bitcast(F16).rearrange("p (r i n) -> p r i n", r=4, i=2)
        gelu = carve(4 * S).rearrange("p (r n) -> p r n", r=4)
        gated = carve(4 * S).rearrange("p (r n) -> p r n", r=4)
        h32 = carve(KT * S).rearrange("p (k n) -> p k n", k=KT)
        hT = [carve(KT * S).bitcast(F16).rearrange("p (i k n) -> p i k n", i=2, k=KT) for _ in range(SLOTS)]
        c32 = carve(2 * SK).rearrange("p (k n) -> p k n", k=2)
        cT = [carve(2 * SK).bitcast(F16).rearrange("p (i k n) -> p i k n", i=2, k=2) for _ in range(SLOTS)]
        arena_words = taken[0]
        inner = [sb(f"inner_{i}", [P, 4, S], F32R) for i in ("high", "low")]

        xin = [sb(f"xin{s}", [P, TT, D], F32) for s in range(SLOTS)]
        xres = [sb(f"xres{s}", [P, TT, D], F32) for s in range(SLOTS)]
        xhat = [sb(f"xhat{s}", [P, TT, D], F32) for s in range(SLOTS)]
        stat6 = sb("stat6", [P, TT, 6], F32)
        moments = [sb(f"moments{s}", [P, TT, 2], F32) for s in range(SLOTS)]
        spread = [sb(f"spread{s}", [P, 2, TT], F32) for s in range(SLOTS)]
        cin = [sb(f"cin{s}", [P, DC], F32) for s in range(SLOTS)]
        peak = sb("peak", [P, 2, 4], F32)
        shift = sb("shift", [P, 2, 4], F32)
        total = sb("total", [P, 2, 4], F32)
        share = sb("share", [P, 2, 4], F32)

        score_ps = stack.enter_context(nc.psum_tensor("score_ps", [P, 2, 2, 512], F32))
        group_ps = stack.enter_context(nc.psum_tensor("group_ps", [P, RING, 512], F32))

        small_in = sem("small_in")
        staged = {n: sem(f"staged_{n}") for n in WEIGHTS + ["ff2", "ctx"]}
        const_ready = sem("const_ready")
        w2_ready = sem("w2_ready")
        setup = sem("setup")
        largest_ready = sem("largest_ready")
        vecs_turned = sem("vecs_turned")
        turned = sem("turned")
        diag_ready = sem("diag_ready")
        spread_out = sem("spread_out")
        scales_ready = sem("scales_ready")
        w_high = sem("w_high")
        w_ready = sem("w_ready")
        pool_past = sem("pool_past")
        dve_past = sem("dve_past")
        x_loaded = [sem(f"x_loaded{s}") for s in range(SLOTS)]
        c_loaded = [sem(f"c_loaded{s}") for s in range(SLOTS)]
        stored = [sem(f"stored{s}") for s in range(SLOTS)]
        stat_step = sem("stat_step")
        stats_ready = sem("stats_ready")
        root_step = sem("root_step")
        root_ready = sem("root_ready")
        xhat_ready = sem("xhat_ready")
        x_biased = [sem(f"x_biased{s}") for s in range(SLOTS)]
        group_full = sem("group_full")
        group_done = sem("group_done")
        group_high = sem("group_high")
        h_high = sem("h_high")
        h_ready = sem("h_ready")
        c_high = sem("c_high")
        c_ready = sem("c_ready")
        scores_full = sem("scores_full")
        peak_ready = sem("peak_ready")
        shift_ready = sem("shift_ready")
        exp_done = sem("exp_done")
        share_ready = sem("share_ready")
        probs_ready = sem("probs_ready")
        probsT_high = sem("probsT_high")
        gelu_done = sem("gelu_done")
        gated_ready = sem("gated_ready")
        inner_high = sem("inner_high")
        inner_ready = sem("inner_ready")
        inner_used = sem("inner_used")
        result_ready = sem("result_ready")

        SMALL = 10
        x_view = x.rearrange("n (t p) d -> n p t d", p=P)
        out_view = out.rearrange("n (t p) d -> n p t d", p=P)

        stage, at = {}, 0
        for n in ["ff2", "wq1", "wk1", "wv1", "wo1", "wq2", "wk2", "wv2", "ff1"]:
            words = 16 * FF // 4 if n == "ff1" else 8 * DA // 4
            stage[n] = arena[:, at:at + words]
            at += words
        stage["wo2"] = stage["ff2"]
        assert max(at + 4 * DC, arena_words) <= ARENA
        view = {n: w[n].rearrange("(k p) n -> p k n", p=kp.get(n, P)) for n in WEIGHTS + ["ff2"]}
        LOADS = ["ff2", "wq1", "wk1", "wv1", "wo1", "wq2", "wk2", "wv2", "ff1", "wo2"]

        ctx_all = arena[:, at:at + 4 * DC].rearrange("p (n d) -> p n d", n=4)
        CCH = NB // 4
        ctx_max = sb("ctx_max", [P, CCH], F32)
        ctx_seen = sem("ctx_seen")

        def st(n):
            return stage[n].rearrange("p (k n) -> p k n", k=view[n].shape[1])

        def weight(n, i, k, a, z):
            return wsb[n][0:kp[n], i, k, a:z]

        THREE = ((0, 0), (0, 1), (1, 0))

        def proj_place(kind, s, j, bank, i):
            if kind in ("q1", "k1", "q2"):
                return qkv[s, kind[0]][:, i, 2 * j:2 * j + 2, :], bank.rearrange("p (m n) -> p m n", m=2), Q_SHIFT
            if kind == "v1":
                return qkv[s, "v"][:, i, j // 2, j % 2 * 512:j % 2 * 512 + 512], bank, Q_SHIFT
            if kind == "k2":
                return (qkv[s, "k"][:, i, 4 * j:4 * j + 4, 0:SK],
                        bank[:, 0:4 * SK].rearrange("p (m n) -> p m n", m=4), C_SHIFT)
            return qkv[s, "v"][0:SK, i, 0, j * 512:j * 512 + 512], bank[0:SK], C_SHIFT

        block = stack.enter_context(nc.Block())

        @block.sync
        def _(sp):
            for i in range(3):
                for c, v in enumerate((g[i], b[i])):
                    at = (2 * i + c) * KT
                    sp.dma_start(vec_rows[at:at + KT, :], v.rearrange("(k p) -> k p", p=P)).then_inc(small_in, 16)
                sp.dma_start(bias_rows[:, i, :], bo[i].partition_broadcast(P)).then_inc(small_in, 16)
            sp.dma_start(vec_rows[6 * KT:NVEC, :], b_ff1.rearrange("(m p) -> m p", p=P)).then_inc(small_in, 16)

            def load(turn):
                for s in range(SLOTS):
                    sp.dma_start(xin[s][:], x_view[turn * SLOTS + s]).then_inc(x_loaded[s], 16)
                    sp.dma_start(cin[s][0:SK, :], ctx[turn * SLOTS + s]).then_inc(c_loaded[s], 16)

            load(0)
            for s in range(SLOTS):
                sp.sem_inc(stored[s], 16)
            for n in LOADS:
                if n == "wo2":
                    sp.wait_ge(w2_ready, 2)
                sp.dma_start(st(n)[0:kp.get(n, P)], view[n]).then_inc(staged[n], 16)
                if n == "ff2":
                    for c in range(CCH):
                        if c:
                            sp.wait_ge(ctx_seen, c)
                        sp.dma_start(ctx_all[0:SK], ctx[4 * c:4 * c + 4].rearrange("n s d -> s n d")).then_inc(staged["ctx"], 16)

            def store(turn):
                for s in range(SLOTS):
                    sp.wait_ge(result_ready, turn * SLOTS + s + 1 + SLOTS)
                    sp.dma_start(out_view[turn * SLOTS + s], xres[s][:]).then_inc(stored[s], 16)

            with sp.Fori(0, TURNS_OF_LOOP - 1) as turn:
                for s in range(SLOTS):
                    sp.wait_ge(x_biased[s], turn * 3 + 1)
                    sp.dma_start(xin[s][:], x_view[turn * SLOTS + SLOTS + s]).then_inc(x_loaded[s], 16)
                for s in range(SLOTS):
                    sp.wait_ge(group_full, group_of(turn, ("ctx", s)) + 1)
                    sp.dma_start(cin[s][0:SK, :], ctx[turn * SLOTS + SLOTS + s]).then_inc(c_loaded[s], 16)
                store(turn)
            for s in range(SLOTS):
                sp.sem_inc(x_loaded[s], 16)
            store(TURNS_OF_LOOP - 1)
            for s in range(SLOTS):
                sp.wait_ge(stored[s], 16 * TURNS_OF_LOOP + 16)

        @block.gpsimd
        def _(pool):
            nc.gpsimd.memset(ones[:], 1.0).then_inc(const_ready, 1)
            nc.gpsimd.memset(half[:], -0.5).then_inc(const_ready, 1)
            nc.gpsimd.memset(largest[:], 0.0).then_inc(const_ready, 1)
            nc.gpsimd.memset(ident[:], 0.0).then_inc(const_ready, 1)
            pool.wait_ge(const_ready, 4)
            nc.gpsimd.affine_select(out=ident[:], in_=ident[:], compare_op=ALU.not_equal, fill=1.0, base=0,
                                    pattern=[[-1, P]], channel_multiplier=1).then_inc(const_ready, 1)
            pool.wait_ge(const_ready, 5)
            pool.wait_ge(small_in, 16 * SMALL)

            def root(turn, s, n):
                i = ln_of(turn, s, n)
                pool.wait_ge(stats_ready, i + 1 + 1)
                pool.sem_inc(pool_past, 1)
                nc.gpsimd.tensor_scalar(spread[s][:, 0, :], moments[s][:, :, 1], EPS, None, ALU.add).then_inc(root_step, 1)
                pool.wait_ge(root_step, i + 1)
                nc.gpsimd.tensor_tensor(spread[s][:, 1, :], spread[s][:, 0, :], half[:], ALU.pow).then_inc(root_ready, 1)

            def add_bias(turn, s, n):
                rows = xin[s] if n == 1 else xres[s]
                if n == 1:
                    pool.wait_ge(stored[s], turn * 16 + 16)
                pool.wait_ge(xhat_ready, turn * NLN + LN_BEFORE[s, 1] + 1 if n == 1 else ln_of(turn, s, n) + 1)
                nc.gpsimd.tensor_tensor(xres[s][:], rows[:], bias_rows[:, n - 1:n, :].to_broadcast([P, TT, D]), ALU.add).then_inc(x_biased[s], 1)

            def normalise(turn, p):
                _, a, _ = of_pair(p)
                K = S if a == 1 else SK
                pool.wait_ge(share_ready, turn * NPAIR + p + 1)
                pool.sem_inc(pool_past, 1)
                for h in range(2):
                    for t in range(TT):
                        rows = probs[:, p % 4, h, t, 0:K]
                        nc.gpsimd.tensor_scalar(rows, rows, share[:, p % 2, 2 * h + t:2 * h + t + 1], 2.0 ** BOUND,
                                                ALU.mult, ALU.mult).then_inc(probs_ready, 1)

            for step in BEFORE:
                if step[0] == "stats":
                    root(None, *step[1:])
            with pool.Fori(0, TURNS_OF_LOOP) as turn:
                for step in ORDER:
                    if step[0] == "stats":
                        root(turn, *step[1:])
                    elif step[0] == "bias":
                        add_bias(turn, step[1], 1)
                    elif step[0] == "rows" and step[2] > 1:
                        add_bias(turn, *step[1:])
                    elif step[0] == "norm":
                        normalise(turn, step[1])

        @block.scalar
        def _(act):
            act.wait_ge(scales_ready, 1)
            for n in WEIGHTS:
                act.wait_ge(staged[n], 16)
                nc.scalar.activation(wsb[n][0:kp[n], 0], st(n)[0:kp[n]], ACT.Copy, scale=up[0:kp[n], COL[n]:COL[n] + 1]).then_inc(w_high, 1)

            def group(turn, step):
                act.wait_ge(group_full, group_of(turn, step) + 1)
                return group_ps[:, bank_of(turn, step), :]

            def h_halves(turn, s, n):
                act.wait_ge(group_done, group_of(turn, ("turn", s, n)) + 1 + RING)
                nc.scalar.activation(hT[s][:, 0], h32[:], ACT.Copy).then_inc(h_high, 1)

            def c_halves(turn, s):
                act.wait_ge(group_done, group_of(turn, ("ctx", s)) + 1 + RING)
                nc.scalar.activation(cT[s][0:KC, 0], c32[0:KC], ACT.Copy).then_inc(c_high, 1)

            def proj(turn, step):
                _, s, kind, j = step
                bank = group(turn, step)
                dst, src, shift_bits = proj_place(kind, s, j, bank, 0)
                nc.scalar.activation(dst, src, ACT.Copy, scale=2.0 ** -shift_bits).then_inc(group_high, 1)

            def exponentials(turn, p):
                _, a, _ = of_pair(p)
                K = S if a == 1 else SK
                act.wait_ge(shift_ready, turn * NPAIR + p + 1)
                for h in range(2):
                    for t in range(TT):
                        i = 2 * h + t
                        ins = nc.scalar.activation(probs[:, p % 4, h, t, 0:K], score_ps[:, p % 2, h, t * K:t * K + K], ACT.Exp,
                                                   scale=score_scale[a], bias=shift[:, p % 2, i:i + 1],
                                                   accum_out=total[:, p % 2, i:i + 1])
                ins.then_inc(exp_done, 1)

            def probs_high(turn, p):
                K = S if p < 2 * PAIRS else SK
                R = P if p < 2 * PAIRS else SK
                for u in units(p):
                    bank = group(turn, ("probs", u))
                    nc.scalar.activation(probsT[0:R, u % 4, 0, :], bank[0:R], ACT.Copy).then_inc(probsT_high, 1)

            def mix(turn, step):
                _, _, j = of_pair(step[1])
                bank = group(turn, step)
                nc.scalar.activation(mixed[:, 0, j, :], bank[:, 0:S], ACT.Copy, scale=2.0 ** -BOUND).then_inc(group_high, 1)

            def gated_done(turn, s, j):
                if s == A:
                    act.wait_ge(gated_ready, turn * FT + j + 1)
                else:
                    act.wait_ge(group_done, group_of(turn, ("ff1", s, j)) + 1 + RING)

            def gate(turn, step):
                _, s, j = step
                if s == A:
                    act.wait_ge(group_done, group_of(turn, ("ff1", s, j)) + 1 + RING)
                    src = raw[:, j, S:2 * S]
                else:
                    src = group(turn, ("ff1", s, j))[:, S:2 * S]
                if j >= 4:
                    gated_done(turn, s, j - 4)
                nc.scalar.activation(gelu[:, j % 4, :], src, ACT.Gelu, scale=ff_scale,
                                     bias=ffb[:, FT + j:FT + j + 1]).then_inc(gelu_done, 1)

            def inner_high_half(turn, step):
                _, s, i = step
                gated_done(turn, s, 2 * i + 1)
                act.wait_ge(inner_used, turn * (NTILE // 2) + s * (FT // 2) + i + 1)
                nc.scalar.activation(inner[0][:, 2 * i % 4:2 * i % 4 + 2, :], gated[:, 2 * i % 4:2 * i % 4 + 2, :], ACT.Copy).then_inc(inner_high, 1)

            for step in BEFORE:
                if step[0] == "turn":
                    h_halves(None, *step[1:])
            with act.Fori(0, TURNS_OF_LOOP) as turn:
                for step in ORDER:
                    if step[0] == "turn":
                        h_halves(turn, *step[1:])
                    elif step[0] == "ctx":
                        c_halves(turn, step[1])
                    elif step[0] == "proj":
                        proj(turn, step)
                    elif step[0] == "exp":
                        exponentials(turn, step[1])
                    elif step[0] == "split_probs":
                        probs_high(turn, step[1])
                    elif step[0] == "mix":
                        mix(turn, step)
                    elif step[0] == "gate":
                        gate(turn, step)
                    elif step[0] == "inner":
                        inner_high_half(turn, step)

        @block.vector
        def _(dve):
            count = [0]

            def link(ins):
                count[0] += 1
                ins.then_inc(setup, 1)
                dve.wait_ge(setup, count[0])

            dve.wait_ge(staged["ff2"], 16)
            nc.vector.tensor_copy(w2sb[0][:], st("ff2")).then_inc(w2_ready, 1)
            dve.wait_ge(w2_ready, 1)
            nc.vector.tensor_tensor(w2sb[1][:], st("ff2"), w2sb[0][:].bitcast(F32), ALU.subtract).then_inc(w2_ready, 1)
            dve.wait_ge(w2_ready, 2)
            dve.wait_ge(const_ready, 5)
            for c in range(CCH):
                dve.wait_ge(staged["ctx"], 16 * (c + 1))
                nc.vector.tensor_reduce(ctx_max[0:SK, c:c + 1], ctx_all[0:SK], AX.XY, ALU.max, apply_absolute_value=True).then_inc(ctx_seen, 1)
            dve.wait_ge(ctx_seen, CCH)
            link(nc.vector.tensor_reduce(largest[0:SK, COL["ctx"]:COL["ctx"] + 1], ctx_max[0:SK], AX.X, ALU.max))
            dve.wait_ge(vecs_turned, 1)
            link(nc.vector.tensor_copy(vecs[:], group_ps[:, 1, 0:NVEC]))
            for i in range(3):
                for c, n in enumerate(("h", "b")):
                    k = COL[f"{n}{i + 1}"]
                    link(nc.vector.tensor_reduce(largest[:, k:k + 1], gains[:, i, c, :], AX.X, ALU.max, apply_absolute_value=True))
            for n in WEIGHTS:
                dve.wait_ge(staged[n], 16)
                link(nc.vector.tensor_reduce(largest[0:kp[n], COL[n]:COL[n] + 1], st(n)[0:kp[n]], AX.XY, ALU.max, apply_absolute_value=True))
            dve.sem_inc(largest_ready, 1)
            dve.wait_ge(turned, 1)
            link(nc.vector.tensor_reduce(top[:], group_ps[0:NCOL, 0, 0:P], AX.X, ALU.max))
            nc.vector.tensor_scalar(diag[:], ident[0:NCOL, 0:NCOL], top[:, 0:1], None, ALU.mult).then_inc(diag_ready, 1)
            dve.wait_ge(spread_out, 1)
            link(nc.vector.tensor_copy(bound[:], group_ps[:, 1, 0:NCOL]))
            h, hb = COL["h1"], COL["b1"]
            link(nc.vector.tensor_tensor(bound[:, h:h + 3], bound[:, h:h + 3], bound[:, hb:hb + 3], ALU.add))
            link(nc.vector.tensor_scalar(bound[:, h:h + 3], bound[:, h:h + 3], float(D) ** 0.5, None, ALU.mult))
            link(nc.vector.tensor_scalar(bound[:], bound[:], FLOOR, None, ALU.max))
            link(nc.vector.tensor_scalar(power[:].bitcast(I32), bound[:].bitcast(I32), EXPONENT, None, ALU.bitwise_and))
            link(nc.vector.reciprocal(up[:], power[:]))
            link(nc.vector.tensor_scalar(up[:], up[:], 2.0 ** (BOUND - 1), None, ALU.mult))
            link(nc.vector.tensor_scalar(down[:], power[:], 2.0 ** (1 - BOUND), None, ALU.mult))

            def times(dst, one, two, factor):
                link(nc.vector.scalar_tensor_tensor(dst, one, factor, two, ALU.mult, ALU.mult))

            def d(n):
                return down[:, COL[n]:COL[n] + 1]

            def u(n):
                return up[:, COL[n]:COL[n] + 1]

            times(part[:, 0:1], d("h1"), d("wq1"), 2.0 ** Q_SHIFT)
            times(part[:, 1:2], d("h1"), d("wk1"), 2.0 ** Q_SHIFT)
            times(score_scale[1], part[:, 0:1], part[:, 1:2], SCALE)
            times(part[:, 2:3], d("h2"), d("wq2"), 2.0 ** Q_SHIFT)
            times(part[:, 3:4], d("ctx"), d("wk2"), 2.0 ** C_SHIFT)
            times(score_scale[2], part[:, 2:3], part[:, 3:4], SCALE)
            for a in (1, 2):
                link(nc.vector.tensor_scalar(score_minus[a], score_scale[a], -1.0, None, ALU.mult))
            times(part[:, 0:1], d("h1"), d("wv1"), 2.0 ** Q_SHIFT)
            times(out_scale[1], part[:, 0:1], d("wo1"), 1.0)
            times(part[:, 1:2], d("ctx"), d("wv2"), 2.0 ** C_SHIFT)
            times(out_scale[2], part[:, 1:2], d("wo2"), 1.0)
            times(ff_scale, d("h3"), d("ff1"), 1.0)
            times(ff_up, u("h3"), u("ff1"), 1.0)
            link(nc.vector.tensor_scalar(ffb_a[:], ffb[:, 0:FT], ff_up, None, ALU.mult))
            for i in range(3):
                link(nc.vector.tensor_scalar(gains_s[:, i], gains[:, i], u(f"h{i + 1}"), None, ALU.mult))
            dve.sem_inc(scales_ready, 1)
            for i, n in enumerate(WEIGHTS):
                dve.wait_ge(w_high, i + 1)
                nc.vector.scalar_tensor_tensor(wsb[n][0:kp[n], 1], st(n)[0:kp[n]], up[0:kp[n], COL[n]:COL[n] + 1], wsb[n][0:kp[n], 0],
                                               ALU.mult, ALU.subtract).then_inc(w_ready, 1)
            dve.sem_inc(group_done, RING)
            dve.sem_inc(result_ready, SLOTS)
            dve.sem_inc(stats_ready, 1)
            dve.sem_inc(h_ready, 1)
            dve.sem_inc(inner_ready, 2)

            def group(turn, step):
                dve.wait_ge(group_full, group_of(turn, step) + 1)
                return group_ps[:, bank_of(turn, step), :]

            def stats(turn, s, n):
                i = ln_of(turn, s, n)
                if n == 1:
                    dve.wait_ge(x_loaded[s], 16 if turn is None else turn * 16 + 32)
                else:
                    dve.wait_ge(group_done, group_of(turn, ("out", s, n - 1, TT - 1)) + 1 + RING)
                rows = xin[s] if n == 1 else xres[s]
                dve.wait_ge(stats_ready, i + 1)
                for t in range(TT):
                    ins = nc.vector.bn_stats(stat6[:, t, :], rows[:, t, :])
                ins.then_inc(stat_step, 1)
                dve.wait_ge(stat_step, i + 1)
                dve.sem_inc(dve_past, 1)
                for t in range(TT):
                    ins = nc.vector.bn_aggr(moments[s][:, t, :], stat6[:, t, :])
                ins.then_inc(stats_ready, 1)

            def normal_rows(turn, s, n):
                dve.wait_ge(root_ready, ln_of(turn, s, n) + 1)
                rows = xin[s] if n == 1 else xres[s]
                for t in range(TT):
                    ins = nc.vector.tensor_scalar(xhat[s][:, t, :], rows[:, t, :], moments[s][:, t, 0:1], spread[s][:, 1, t:t + 1],
                                                  ALU.subtract, ALU.mult)
                ins.then_inc(xhat_ready, 1)

            def h_halves(turn, step):
                _, s, n = step
                dve.wait_ge(h_ready, ln_of(turn, s, n) + 1)
                bank = group(turn, step)
                for k in range(KT):
                    ins = nc.vector.tensor_scalar(h32[:, k, :], bank[:, k * S:k * S + S], gains_s[:, n - 1, 0, k:k + 1],
                                                  gains_s[:, n - 1, 1, k:k + 1], ALU.mult, ALU.add)
                ins.then_inc(group_done, 1)
                dve.wait_ge(h_high, ln_of(turn, s, n) + 1)
                nc.vector.tensor_tensor(hT[s][:, 1], h32[:], hT[s][:, 0], ALU.subtract).then_inc(h_ready, 1)

            def c_halves(turn, step):
                _, s = step
                bank = group(turn, step)
                nc.vector.tensor_scalar(c32[0:KC], bank[0:KC, 0:2 * SK].rearrange("p (k n) -> p k n", k=2), u("ctx")[0:KC], None,
                                        ALU.mult).then_inc(group_done, 1)
                dve.wait_ge(c_high, turn * SLOTS + CTXS[s] + 1)
                nc.vector.tensor_tensor(cT[s][0:KC, 1], c32[0:KC], cT[s][0:KC, 0], ALU.subtract).then_inc(c_ready, 1)

            def low(turn, step, dst, src, high, factor):
                dve.wait_ge(group_high, turn * NHIGH + HIGH[step] + 1)
                nc.vector.scalar_tensor_tensor(dst, src, factor, high, ALU.mult, ALU.subtract).then_inc(group_done, 1)

            def proj(turn, step):
                _, s, kind, j = step
                bank = group_ps[:, bank_of(turn, step), :]
                high, src, shift_bits = proj_place(kind, s, j, bank, 0)
                dst, _, _ = proj_place(kind, s, j, bank, 1)
                low(turn, step, dst, src, high, 2.0 ** -shift_bits)

            def mix(turn, step):
                _, _, j = of_pair(step[1])
                low(turn, step, mixed[:, 1, j, :], group_ps[:, bank_of(turn, step), 0:S], mixed[:, 0, j, :], 2.0 ** -BOUND)

            def maxima(turn, p):
                _, a, _ = of_pair(p)
                K = S if a == 1 else SK
                dve.wait_ge(scores_full, turn * NPAIR + p + 1)
                nc.vector.tensor_reduce(peak[:, p % 2, :].rearrange("p (h t) -> p h t", h=2),
                                        score_ps[:, p % 2, :, 0:TT * K].rearrange("p h (t k) -> p h t k", t=TT),
                                        AX.X, ALU.max).then_inc(peak_ready, 1)
                dve.wait_ge(peak_ready, turn * NPAIR + p + 1)
                nc.vector.tensor_scalar(shift[:, p % 2, :], peak[:, p % 2, :], score_minus[a], None, ALU.mult).then_inc(shift_ready, 1)

            def shares(turn, p):
                dve.wait_ge(exp_done, turn * NPAIR + p + 1)
                nc.vector.reciprocal(share[:, p % 2, :], total[:, p % 2, :]).then_inc(share_ready, 1)

            def probs_low(turn, p):
                R = P if p < 2 * PAIRS else SK
                for unit in units(p):
                    dve.wait_ge(probsT_high, turn * NUNIT + unit + 1)
                    bank = group_ps[:, bank_of(turn, ("probs", unit)), :]
                    nc.vector.tensor_tensor(probsT[0:R, unit % 4, 1, :], bank[0:R], probsT[0:R, unit % 4, 0, :],
                                            ALU.subtract).then_inc(group_done, 1)

            def residual(turn, step):
                _, s, n, t = step
                bank = group(turn, step)
                dve.wait_ge(x_biased[s], turn * 3 + n)
                nc.vector.scalar_tensor_tensor(xres[s][:, t, :], bank[:, 0:D], out_scale[n], xres[s][:, t, :],
                                               ALU.mult, ALU.add).then_inc(group_done, 1)

            def keep_products(turn, step):
                _, s, j = step
                bank = group(turn, step)
                nc.vector.tensor_copy(raw[:, j, :], bank).then_inc(group_done, 1)

            def gate(turn, step):
                _, s, j = step
                pairs_before = turn * (NTILE // 2) + s * (FT // 2) + j // 2
                dve.wait_ge(inner_ready, pairs_before + 1)
                dve.wait_ge(gelu_done, turn * NTILE + s * FT + j + 1)
                src, done = (raw[:, j, 0:S], gated_ready) if s == A else (group_ps[:, bank_of(turn, ("ff1", s, j)), 0:S], group_done)
                nc.vector.scalar_tensor_tensor(gated[:, j % 4, :], src, ffb_a[:, j:j + 1], gelu[:, j % 4, :],
                                               ALU.add, ALU.mult).then_inc(done, 1)

            def inner_low_half(turn, step):
                _, s, i = step
                dve.wait_ge(inner_high, turn * (NTILE // 2) + s * (FT // 2) + i + 1)
                two = slice(2 * i % 4, 2 * i % 4 + 2)
                nc.vector.tensor_tensor(inner[1][:, two, :], gated[:, two, :], inner[0][:, two, :].bitcast(F32),
                                        ALU.subtract).then_inc(inner_ready, 1)

            def finish(turn, s):
                dve.wait_ge(inner_used, turn * (NTILE // 2) + (s + 1) * (FT // 2) + 2)
                dve.wait_ge(x_biased[s], turn * 3 + 3)
                ins = nc.vector.scalar_tensor_tensor(xres[s][:], score_ps[:, s, :, 0:D], ff_scale, xres[s][:], ALU.mult, ALU.add)
                ins.then_inc(result_ready, 1)

            for step in BEFORE:
                if step[0] == "stats":
                    stats(None, *step[1:])
                elif step[0] == "rows":
                    normal_rows(None, *step[1:])
                elif step[0] == "turn":
                    h_halves(None, step)
            with dve.Fori(0, TURNS_OF_LOOP) as turn:
                for step in ORDER:
                    if step[0] == "stats":
                        stats(turn, *step[1:])
                    elif step[0] == "rows":
                        normal_rows(turn, *step[1:])
                    elif step[0] == "turn":
                        h_halves(turn, step)
                    elif step[0] == "ctx":
                        c_halves(turn, step)
                    elif step[0] == "proj":
                        proj(turn, step)
                    elif step[0] == "scores":
                        maxima(turn, step[1])
                    elif step[0] == "norm":
                        shares(turn, step[1])
                    elif step[0] == "split_probs":
                        probs_low(turn, step[1])
                    elif step[0] == "mix":
                        mix(turn, step)
                    elif step[0] == "out":
                        residual(turn, step)
                    elif step[0] == "ff1" and step[1] == A:
                        keep_products(turn, step)
                    elif step[0] == "gate":
                        gate(turn, step)
                    elif step[0] == "inner":
                        inner_low_half(turn, step)
                    elif step[0] == "finish":
                        finish(turn, step[1])

        @block.tensor
        def _(pe):
            pe.wait_ge(const_ready, 5)
            pe.wait_ge(small_in, 16 * SMALL)
            nc.tensor.transpose(group_ps[:, 1, 0:NVEC], vec_rows[:], ident[0:NVEC, 0:NVEC]).then_inc(vecs_turned, 1)
            pe.wait_ge(largest_ready, 1)
            nc.tensor.transpose(group_ps[0:NCOL, 0, 0:P], largest[:], ident[:]).then_inc(turned, 1)
            pe.wait_ge(diag_ready, 1)
            nc.tensor.matmul(group_ps[:, 1, 0:NCOL], ones[:], diag[:], start=True, stop=True).then_inc(spread_out, 1)
            pe.wait_ge(w_ready, len(WEIGHTS))
            pe.sem_inc(inner_used, 2)

            def done(turn, *steps):
                pe.wait_ge(group_done, group_of(turn, max(steps, key=GROUP.get)) + 1 + RING)

            def group(turn, step, *after):
                if max([GROUP[x] + RING for x in after], default=-1) > GROUP.get(step, 0):
                    done(turn, *after)
                else:
                    pe.wait_ge(group_done, group_of(turn, step) + 1)
                return group_ps[:, bank_of(turn, step), :]

            def turn_rows(turn, step):
                _, s, n = step
                pe.wait_ge(xhat_ready, ln_of(turn, s, n) + 1)
                bank = group(turn, step)
                for k in range(KT):
                    for t in range(TT):
                        ins = nc.tensor.transpose(bank[:, k * S + t * P:k * S + t * P + P], xhat[s][:, t, k * P:k * P + P], ident[:])
                ins.then_inc(group_full, 1)

            def turn_ctx(turn, step):
                _, s = step
                pe.wait_ge(c_loaded[s], turn * 16 + 16)
                bank = group(turn, step)
                for k in range(2):
                    ins = nc.tensor.transpose(bank[0:KC, k * SK:k * SK + SK], cin[s][0:SK, k * KC:k * KC + KC], ident[0:SK, 0:SK])
                ins.then_inc(group_full, 1)

            def proj(turn, step):
                _, s, kind, j = step
                if kind[1] == "1":
                    pe.wait_ge(h_ready, turn * NLN + LN_BEFORE[s, 1] + 2)
                elif kind == "q2":
                    pe.wait_ge(h_ready, ln_of(turn, s, 2) + 2)
                else:
                    pe.wait_ge(c_ready, turn * SLOTS + CTXS[s] + 1)
                bank = group(turn, step)
                name = "w" + kind
                if kind in ("q1", "k1", "q2", "k2"):
                    src = cT[s][0:KC] if kind == "k2" else hT[s]
                    n, per = (SK, 4) if kind == "k2" else (S, 2)
                    for m in range(per):
                        mt = per * j + m
                        for k in range(2):
                            for i, (a, z) in enumerate(THREE):
                                ins = nc.tensor.matmul(bank[:, m * n:m * n + n], weight(name, z, k, mt * P, mt * P + P), src[:, a, k, :],
                                                       start=(k == 0 and i == 0), stop=(k == 1 and i == 2))
                else:
                    t, c = (j // 2, j % 2) if kind == "v1" else (0, j)
                    M = P if kind == "v1" else SK
                    src = hT[s] if kind == "v1" else cT[s][0:KC]
                    for k in range(2):
                        for i, (a, z) in enumerate(THREE):
                            ins = nc.tensor.matmul(bank[0:M], src[:, a, k, t * P:t * P + M], weight(name, z, k, c * 512, c * 512 + 512),
                                                   start=(k == 0 and i == 0), stop=(k == 1 and i == 2))
                ins.then_inc(group_full, 1)

            def scores(turn, p):
                s, a, j = of_pair(p)
                done(turn, ("proj", s, f"q{a}", j // 2), ("proj", s, f"k{a}", j // 2 if a == 1 else j // 4))
                if p < 2:
                    pe.wait_ge(result_ready, turn * SLOTS + p + 1)
                else:
                    pe.wait_ge(exp_done, turn * NPAIR + p - 1)
                K = S if a == 1 else SK
                q, k = qkv[s, "q"], qkv[s, "k"]
                for t in range(TT):
                    for i, (a_, z) in enumerate(THREE):
                        for h in range(2):
                            r = slice(h * DH, h * DH + DH)
                            ins = nc.tensor.matmul(score_ps[:, p % 2, h, t * K:t * K + K], q[r, a_, j, t * P:t * P + P], k[r, z, j, 0:K],
                                                   start=(i == 0), stop=(i == 2))
                ins.then_inc(scores_full, 1)

            def turn_probs(turn, p):
                _, a, _ = of_pair(p)
                pe.wait_ge(probs_ready, turn * (4 * NPAIR) + 4 * (p + 1))
                for h in range(2):
                    u = units(p)[h if a == 1 else 0]
                    if a == 1 or h == 0:
                        bank = group(turn, ("probs", u))
                    for k in range(TT if a == 1 else 1):
                        K = P if a == 1 else SK
                        for t in range(TT):
                            at = (k if a == 1 else h) * S + t * P
                            ins = nc.tensor.transpose(bank[0:K, at:at + P], probs[:, p % 4, h, t, k * P:k * P + K], ident[:])
                    if a == 1 or h == 1:
                        ins.then_inc(group_full, 1)

            def mix(turn, step):
                p = step[1]
                s, a, j = of_pair(p)
                values = [("proj", s, "v1", j // 4), ("proj", s, "v1", 2 + j // 4)] if a == 1 else [("proj", s, "v2", j // 4)]
                bank = group(turn, step, ("probs", units(p)[-1]), *values)
                v = qkv[s, "v"]
                kts = TT if a == 1 else 1
                K = P if a == 1 else SK
                for k in range(kts):
                    for i, (a_, z) in enumerate(THREE):
                        for h in range(2):
                            u = units(p)[h if a == 1 else 0]
                            at = (k if a == 1 else h) * S
                            ins = nc.tensor.matmul(bank[h * DH:h * DH + DH, 0:S], v[0:K, z, k, (2 * j + h) * DH:(2 * j + h + 1) * DH],
                                                   probsT[0:K, u % 4, a_, at:at + S], start=(k == 0 and i == 0), stop=(k == kts - 1 and i == 2))
                ins.then_inc(group_full, 1)

            def project_out(turn, step):
                _, s, n, t = step
                last = (n - 1) * 2 * PAIRS + s * PAIRS + PAIRS - 1
                bank = group(turn, step, ("mix", last))
                for c in range(AT):
                    for i, (a, z) in enumerate(THREE):
                        ins = nc.tensor.matmul(bank[:, 0:D], mixed[:, a, c, t * P:t * P + P], wsb[f"wo{n}"][:, z, c, :],
                                               start=(c == 0 and i == 0), stop=(c == AT - 1 and i == 2))
                ins.then_inc(group_full, 1)

            def ff1(turn, step):
                _, s, j = step
                pe.wait_ge(h_ready, ln_of(turn, s, 3) + 2)
                bank = group(turn, step)
                for half_ in (1, 0):
                    at = half_ * FF + j * P
                    for k in range(KT):
                        for i, (a, z) in enumerate(THREE):
                            ins = nc.tensor.matmul(bank[:, half_ * S:half_ * S + S], weight("ff1", z, k, at, at + P), hT[s][:, a, k, :],
                                                   start=(k == 0 and i == 0), stop=(k == KT - 1 and i == 2))
                ins.then_inc(group_full, 1)

            def ff2(turn, step):
                _, s, j = step
                if j == 0:
                    pe.wait_ge(exp_done, turn * NPAIR + NPAIR - 1 + s)
                pe.wait_ge(inner_ready, turn * (NTILE // 2) + s * (FT // 2) + j // 2 + 1 + 2)
                for t in range(TT):
                    for i, (a, z) in enumerate(THREE):
                        ins = nc.tensor.matmul(score_ps[:, s, t, 0:D], inner[a][:, j % 4, t * P:t * P + P], w2sb[z][:, j, :],
                                               start=(j == 0 and i == 0), stop=(j == FT - 1 and i == 2))
                if j % 2:
                    ins.then_inc(inner_used, 1)

            for step in BEFORE:
                if step[0] == "turn":
                    turn_rows(None, step)
            with pe.Fori(0, TURNS_OF_LOOP) as turn:
                for step in ORDER:
                    if step[0] == "turn":
                        turn_rows(turn, step)
                    elif step[0] == "ctx":
                        turn_ctx(turn, step)
                    elif step[0] == "proj":
                        proj(turn, step)
                    elif step[0] == "scores":
                        scores(turn, step[1])
                    elif step[0] == "turn_probs":
                        turn_probs(turn, step[1])
                    elif step[0] == "mix":
                        mix(turn, step)
                    elif step[0] == "out":
                        project_out(turn, step)
                    elif step[0] == "ff1":
                        ff1(turn, step)
                    elif step[0] == "ff2":
                        ff2(turn, step)


def kernel(**inputs):
    import numpy as np
    import concourse.bacc as bacc
    from concourse.bass_utils import run_bass_kernel_spmd

    nc = bacc.Bacc("TRN2", target_bir_lowering=False, num_devices=1, dynamic_dma_scratch_size=2048)
    arrays, aps = {}, {}
    for name, value in inputs.items():
        array = np.ascontiguousarray(value)
        arrays[f"in_{name}"] = array
        aps[name] = nc.dram_tensor(f"in_{name}", array.shape, mybir.dt.from_np(array.dtype), kind="ExternalInput").ap()
    shape = inputs["x"].shape
    out = nc.dram_tensor("out", shape, F32, kind="ExternalOutput").ap()

    def of(name):
        return aps["L0_xattn_" + name]

    w = {n: of(n) for n in WEIGHTS if n != "ff1"}
    w["ff1"], w["ff2"] = of("w_ff1"), of("w_ff2")
    bass_xattn_block(nc, aps["x"], aps["ctx_768"], w, [of(f"g{i}") for i in (1, 2, 3)], [of(f"b{i}") for i in (1, 2, 3)],
                     [of("bo1"), of("bo2"), of("b_ff2")], of("b_ff1"), out)
    result = run_bass_kernel_spmd(nc, [arrays], core_ids=[0])
    return result.results[0]["out"]
```

```python
from contextlib import ExitStack

import concourse.bass as bass
from concourse import mybir

ALU = mybir.AluOpType
ACT = mybir.ActivationFunctionType
AX = mybir.AxisListType
F32, F16, F32R, I32 = mybir.dt.float32, mybir.dt.float16, mybir.dt.float32r, mybir.dt.int32

P = 128
HEADS, DH = 16, 64
PAIRS = HEADS // 2
EPS = 1e-5
SLOTS = 2

BOUND = 14
Q_SHIFT = 18
C_SHIFT = 22
FLOOR = 2.0 ** -20
EXPONENT = 0x7F800000

WEIGHTS = ["wq1", "wk1", "wv1", "wo1", "wq2", "wk2", "wv2", "wo2", "ff1"]
COL = {n: i for i, n in enumerate(WEIGHTS + ["ctx", "h1", "h2", "h3", "b1", "b2", "b3"])}
NCOL = 16


A, B = range(SLOTS)


TABLE = """
k1.A.0 q1.A.0 k1.A.1 q1.B.1
scores.0 max.0 v1.A.1 exp.0
scores.1 q1.A.1 max.1 k1.B.0 k1.A.2 share.0 q1.A.2
scores.2 max.2 exp.1 k1.A.3 v1.A.0 v1.B.2
scores.3 exp.2 share.1 max.3 norm.0 norm.1 share.2 probs.0 v1.A.2 exp.3 norm.2
scores.4 max.4 probs.1 share.3 q1.A.3 v1.B.0 exp.4
scores.5 max.5 q1.B.0 mix.0 probs.2
scores.6 share.4 exp.5 ctx.A share.5 q1.B.2 max.6 norm.3 mix.1 v1.A.3 probs.3
scores.7 norm.4 exp.6 max.7 share.6 k1.B.1 mix.2 probs.4 exp.7
scores.8 max.8 mix.3 k1.B.2 norm.5 probs.5 exp.8
scores.9 max.9 q1.B.3 share.7 mix.4 norm.6 norm.7 probs.6 share.8 norm.8 exp.9
scores.10 max.10 mix.5 v1.B.1 probs.7 share.9
scores.11 exp.10 mix.6 mix.7 probs.8 bias.A share.10 norm.9 max.11 norm.10
scores.12 probs.9 out1.A.1 exp.11 max.12 share.11 k1.B.3 out1.A.0 stats2.A
scores.13 max.13 exp.12 mix.8 rows2.A mix.9 norm.11 probs.10
scores.14 exp.13 turn2.A k2.A.0 share.12 mix.10 bias.B max.14 v1.B.3 share.13 q2.A.1 probs.11 norm.12 exp.14
scores.15 max.15 q2.A.0 probs.12 mix.11 exp.15
scores.16 max.16 share.14 norm.13 probs.13 share.15 norm.14 v2.A.0 k2.A.1 exp.16
scores.17 max.17 mix.12 mix.13 share.16 norm.15 probs.14
scores.18 max.18 exp.17 q2.A.3 probs.15 share.17 q2.A.2
scores.19 max.19 norm.16 exp.18 mix.14 mix.15 probs.16
scores.20 max.20 share.18 exp.19 exp.20 ctx.B norm.17 probs.17 norm.18 share.19 out1.B.1 share.20 out1.B.0 stats2.B
    probs.18
scores.21 max.21 rows2.B mix.16 v2.A.1 mix.17 norm.19 norm.20
scores.22 exp.21 turn2.B max.22 k2.B.0 k2.B.1 probs.19 exp.22
scores.23 share.21 max.23 norm.21 q2.B.0 mix.18 share.22 q2.B.1 probs.20 norm.22 exp.23
scores.24 max.24 share.23 q2.B.3 probs.21 mix.19 probs.22
scores.25 exp.24 max.25 mix.20 norm.23 probs.23 share.24 mix.21 v2.B.0 exp.25
scores.26 max.26 share.25 mix.22 mix.23 q2.B.2 exp.26 norm.24
scores.27 max.27 norm.25 probs.24 exp.27 share.26 norm.26 out2.A.1 share.27
scores.28 max.28 probs.25 out2.A.0 stats3.A
scores.29 max.29 exp.28 share.28 norm.27 probs.26 rows3.A norm.28 mix.24 mix.25 mix.26 exp.29 turn3.A v2.B.1
scores.30 max.30 share.29 probs.27
scores.31 probs.28 exp.30 max.31 ff1.A.0 norm.29 exp.31 share.30 ff1.A.1 ff1.A.2 share.31 mix.27 norm.30 probs.29
    mix.28 ff1.A.3 probs.30 norm.31 probs.31 mix.29 ff1.A.4 mix.30 mix.31 gate.A.0 ff1.A.5 gate.A.1 gate.A.2 out2.B.0
    gate.A.3 inner.A.0 gate.A.4 gate.A.5 out2.B.1 stats3.B inner.A.1 ff1.A.6 ff2.A.0 rows3.B ff2.A.1 inner.A.2 ff2.A.2
    ff2.A.3 turn3.B ff1.A.7 ff2.A.4 ff2.A.5 gate.A.6 ff1.B.0 stats1.A gate.A.7 gate.B.0 stats1.B ff1.B.1 ff1.B.2
    ff1.B.3 gate.B.1 inner.A.3 ff2.A.6 rows1.A ff1.B.4 gate.B.2 gate.B.3 rows1.B ff2.A.7 inner.B.0 gate.B.4 turn1.A
    finish.A ff1.B.5 ff1.B.6 inner.B.1 ff1.B.7 ff2.B.0 gate.B.5 ff2.B.1 gate.B.6 gate.B.7 ff2.B.2 inner.B.2 ff2.B.3
    inner.B.3 turn1.B ff2.B.4 ff2.B.5 ff2.B.6 ff2.B.7 finish.B
"""
PAIR_STEPS = ("scores", "max", "exp", "share", "norm", "probs", "mix")


def read_step(text):
    name, where, *part = text.split(".")
    if name in PAIR_STEPS:
        return name, int(where)
    s, part = "AB".index(where), [int(i) for i in part]
    if name[0] in "qkv":
        return "proj", s, name, part[0]
    if name[:-1] in ("stats", "rows", "turn", "out"):
        return name[:-1], s, int(name[-1]), *part
    return name, s, *part


BEFORE = [(x, s, 1) for x in ("stats", "rows", "turn") for s in range(SLOTS)]
ORDER = [read_step(text) for text in TABLE.split()]
RING = 4


def units(p):
    return [2 * p, 2 * p + 1] if p < 2 * PAIRS else [2 * PAIRS + p]


def groups_of(steps):
    taken = []
    for step in steps:
        if step[0] == "probs":
            taken += [("probs", u) for u in units(step[1])]
        elif step[0] in ("turn", "proj", "ctx", "mix", "out", "ff1"):
            taken.append(step)
    return {step: i for i, step in enumerate(taken)}


def places(*kinds):
    return {step: i for i, step in enumerate(x for x in ORDER if x[0] in kinds)}


GROUP, GROUP_BEFORE = groups_of(ORDER), groups_of(BEFORE)
NGROUP = len(GROUP)
HIGH = places("proj", "mix")
NHIGH = len(HIGH)
LN = {step[1:]: i for step, i in places("stats").items()}
LN_BEFORE = {(s, 1): s for s in range(SLOTS)}
CTXS = {step[1]: i for step, i in places("ctx").items()}
NPAIR = 4 * PAIRS
NUNIT = units(NPAIR - 1)[-1] + 1
NLN = len(LN)
NTILE = 8 * SLOTS
assert NGROUP % RING == 0 and NPAIR % 4 == 0 and NUNIT % 4 == 0
assert all([x[1:] for x in ORDER if x[0] == kind] == list(LN) for kind in ("rows", "turn"))
assert [LN[s, 1] for s in range(SLOTS)] == [NLN - 2, NLN - 1]


def group_of(turn, step):
    return GROUP_BEFORE[step] if turn is None else turn * NGROUP + len(GROUP_BEFORE) + GROUP[step]


def bank_of(turn, step):
    return (GROUP_BEFORE[step] if turn is None else len(GROUP_BEFORE) + GROUP[step]) % RING


def ln_of(turn, s, n):
    return LN_BEFORE[s, n] if turn is None else turn * NLN + len(LN_BEFORE) + LN[s, n]


def of_pair(p):
    return p // PAIRS % 2, p // (2 * PAIRS) + 1, p % PAIRS


def bass_xattn_block(nc, x, ctx, w, g, b, bo, b_ff1, out):
    NB, S, D = x.shape
    SK, DC = ctx.shape[1], ctx.shape[2]
    DA = HEADS * DH
    FF = w["ff2"].shape[0]
    KT, TT, AT = D // P, S // P, DA // P
    FT = FF // P
    REST = DC - P
    TURNS_OF_LOOP = NB // SLOTS
    SCALE = DH ** -0.5
    assert D == 256 and S == 256 and SK <= P and 2 * REST == P and AT == PAIRS and FT == 8

    with ExitStack() as stack:
        def sb(name, shape, dt):
            return stack.enter_context(nc.sbuf_tensor(name, shape, dt))

        def sem(name):
            return stack.enter_context(nc.semaphore(name))

        shape = {n: [2, AT, D] if n in ("wo1", "wo2") else [2, 2, 2 * FF] if n == "ff1" else [2, 2, DA] for n in WEIGHTS}
        wsb = {n: sb(n, [P] + shape[n], F16) for n in WEIGHTS}
        w2sb = [sb(f"w2_{i}", [P, FT, D], F32R) for i in ("high", "low")]
        ident = sb("ident", [P, P], F32)
        ones = sb("ones", [NCOL, P], F32)
        half = sb("half", [P, TT], F32)
        bias_rows = sb("bias_rows", [P, 3, D], F32)
        NVEC = 3 * 2 * KT + 2 * FT
        vec_rows = sb("vec_rows", [NVEC, P], F32)
        vecs = sb("vecs", [P, NVEC], F32)
        gains = vecs[:, 0:6 * KT].rearrange("p (i c k) -> p i c k", i=3, c=2)
        ffb = vecs[:, 6 * KT:NVEC]
        gains_s = sb("gains_s", [P, 3, 2, KT], F32)
        ffb_a = sb("ffb_a", [P, FT], F32)
        largest = sb("largest", [P, NCOL], F32)
        top = sb("top", [NCOL, 1], F32)
        diag = sb("diag", [NCOL, NCOL], F32)
        bound = sb("bound", [P, NCOL], F32)
        power = sb("power", [P, NCOL], F32)
        up = sb("up", [P, NCOL], F32)
        down = sb("down", [P, NCOL], F32)
        sc = sb("sc", [P, 12], F32)
        score_scale = {1: sc[:, 0:1], 2: sc[:, 1:2]}
        score_minus = {1: sc[:, 2:3], 2: sc[:, 3:4]}
        out_scale = {1: sc[:, 4:5], 2: sc[:, 5:6]}
        ff_scale = sc[:, 6:7]
        ff_up = sc[:, 7:8]
        part = sc[:, 8:12]

        ARENA = 97 * 256
        arena = sb("arena", [P, ARENA], F32)
        taken = [0]

        def carve(words):
            at = taken[0]
            taken[0] += words
            return arena[:, at:at + words]

        qkv = {}
        raw = arena[:, 0:2 * AT * S].rearrange("p (j n) -> p j n", j=FT)
        for s in range(SLOTS):
            qkv[s, "q"] = carve(AT * S).bitcast(F16).rearrange("p (i m n) -> p i m n", i=2, m=AT)
            qkv[s, "k"] = carve(AT * S).bitcast(F16).rearrange("p (i m n) -> p i m n", i=2, m=AT)
            qkv[s, "v"] = carve(TT * DA).bitcast(F16).rearrange("p (i t n) -> p i t n", i=2, t=TT)
        mixed = carve(AT * S).bitcast(F16).rearrange("p (i m n) -> p i m n", i=2, m=AT)
        probs = carve(4 * 2 * TT * S).rearrange("p (r h t k) -> p r h t k", r=4, h=2, t=TT)
        probsT = carve(4 * 512).bitcast(F16).rearrange("p (r i n) -> p r i n", r=4, i=2)
        gelu = carve(4 * S).rearrange("p (r n) -> p r n", r=4)
        gated = carve(4 * S).rearrange("p (r n) -> p r n", r=4)
        h32 = carve(KT * S).rearrange("p (k n) -> p k n", k=KT)
        hT = [carve(KT * S).bitcast(F16).rearrange("p (i k n) -> p i k n", i=2, k=KT) for _ in range(SLOTS)]
        c32 = carve(2 * SK).rearrange("p (k n) -> p k n", k=2)
        cT = [carve(2 * SK).bitcast(F16).rearrange("p (i k n) -> p i k n", i=2, k=2) for _ in range(SLOTS)]
        arena_words = taken[0]
        inner = [sb(f"inner_{i}", [P, 4, S], F32R) for i in ("high", "low")]

        xin = [sb(f"xin{s}", [P, TT, D], F32) for s in range(SLOTS)]
        xres = [sb(f"xres{s}", [P, TT, D], F32) for s in range(SLOTS)]
        xhat = [sb(f"xhat{s}", [P, TT, D], F32) for s in range(SLOTS)]
        stat6 = sb("stat6", [P, TT, 6], F32)
        moments = [sb(f"moments{s}", [P, TT, 2], F32) for s in range(SLOTS)]
        spread = [sb(f"spread{s}", [P, 2, TT], F32) for s in range(SLOTS)]
        cin = [sb(f"cin{s}", [P, 2 * P], F32) for s in range(SLOTS)]
        peak = sb("peak", [P, 4, 4], F32)
        shift = sb("shift", [P, 4, 4], F32)
        total = sb("total", [P, 4, 4], F32)
        share = sb("share", [P, 4, 4], F32)

        score_ps = stack.enter_context(nc.psum_tensor("score_ps", [P, 2, 2, 512], F32))
        group_ps = stack.enter_context(nc.psum_tensor("group_ps", [P, RING, 512], F32))

        small_in = sem("small_in")
        staged = {n: sem(f"staged_{n}") for n in WEIGHTS + ["ff2", "ctx"]}
        const_ready = sem("const_ready")
        w2_ready = sem("w2_ready")
        setup = sem("setup")
        ctx_seen = sem("ctx_seen")
        largest_ready = sem("largest_ready")
        vecs_turned = sem("vecs_turned")
        turned = sem("turned")
        diag_ready = sem("diag_ready")
        spread_out = sem("spread_out")
        scales_ready = sem("scales_ready")
        scaled = sem("scaled")
        consts_ready = sem("consts_ready")
        w_high = sem("w_high")
        w_ready = sem("w_ready")
        pool_past = sem("pool_past")
        dve_past = sem("dve_past")
        x_loaded = [sem(f"x_loaded{s}") for s in range(SLOTS)]
        c_loaded = [sem(f"c_loaded{s}") for s in range(SLOTS)]
        stored = [sem(f"stored{s}") for s in range(SLOTS)]
        stat_step = sem("stat_step")
        stats_ready = sem("stats_ready")
        root_step = sem("root_step")
        root_ready = sem("root_ready")
        xhat_ready = sem("xhat_ready")
        x_biased = [sem(f"x_biased{s}") for s in range(SLOTS)]
        group_full = sem("group_full")
        group_done = sem("group_done")
        group_high = sem("group_high")
        h_high = sem("h_high")
        h_ready = sem("h_ready")
        c_high = sem("c_high")
        c_ready = sem("c_ready")
        scores_full = sem("scores_full")
        peak_ready = sem("peak_ready")
        shift_ready = sem("shift_ready")
        exp_done = sem("exp_done")
        share_ready = sem("share_ready")
        probs_ready = sem("probs_ready")
        probsT_high = sem("probsT_high")
        gelu_done = sem("gelu_done")
        gated_ready = sem("gated_ready")
        inner_high = sem("inner_high")
        inner_ready = sem("inner_ready")
        inner_used = sem("inner_used")
        result_ready = sem("result_ready")

        SMALL = 10
        x_view = x.rearrange("n (t p) d -> n p t d", p=P)
        out_view = out.rearrange("n (t p) d -> n p t d", p=P)

        stage, at = {}, 0
        for n in ["ff2", "wq1", "wk1", "wv1", "wo1", "wq2", "wk2", "wv2", "wo2", "ff1"]:
            words = 16 * FF // 4 if n == "ff1" else 8 * DA // 4
            stage[n] = arena[:, at:at + words]
            at += words
        CTX_WORDS = NB * SK * DC // P
        assert max(at, arena_words) <= ARENA and CTX_WORDS <= ARENA - 8 * (8 * DA // 4)
        view = {n: w[n].rearrange("(k p) n -> p k n", p=P) for n in WEIGHTS + ["ff2"] if n not in ("wk2", "wv2")}
        ctx_all = arena[:, ARENA - CTX_WORDS:ARENA]
        ctx_view = ctx.rearrange("n s d -> (n s d)").rearrange("(p m) -> p m", p=P)
        PHASES = [["wq1", "wk1", "wv1", "wo1", "wq2"], ["ff1", "wk2", "wv2", "wo2"]]
        LOADS = PHASES[0] + ["ff1", "ff2", "wk2", "wv2", "wo2"]
        SPLIT = PHASES[0] + PHASES[1]
        COLUMNS = [(0, len(PHASES[0])), (len(PHASES[0]), NCOL)]
        LOW_BY_POOL = ("wo1",)
        assert [COL[n] for n in PHASES[0]] == list(range(len(PHASES[0])))

        def st(n):
            return stage[n].rearrange("p (k n) -> p k n", k=w[n].shape[0] // P if n in view else 2)

        def weight(n, i, k, a, z, rows=P):
            return wsb[n][0:rows, i, k, a:z]

        THREE = ((0, 0), (0, 1), (1, 0))
        CTX_PRODUCTS = [(0, 0, 0, P), (0, 1, 0, P), (1, 0, 0, P), (0, 0, 1, P), (0, 1, 1, REST)]

        def proj_place(kind, s, j, bank, i):
            if kind in ("q1", "k1", "q2"):
                return qkv[s, kind[0]][:, i, 2 * j:2 * j + 2, :], bank.rearrange("p (m n) -> p m n", m=2), Q_SHIFT
            if kind == "v1":
                return qkv[s, "v"][:, i, j // 2, j % 2 * 512:j % 2 * 512 + 512], bank, Q_SHIFT
            if kind == "k2":
                return (qkv[s, "k"][:, i, 4 * j:4 * j + 4, 0:SK],
                        bank[:, 0:4 * SK].rearrange("p (m n) -> p m n", m=4), C_SHIFT)
            return qkv[s, "v"][0:SK, i, 0, j * 512:j * 512 + 512], bank[0:SK], C_SHIFT

        block = stack.enter_context(nc.Block())

        @block.sync
        def _(sp):
            for i in range(3):
                for c, v in enumerate((g[i], b[i])):
                    at = (2 * i + c) * KT
                    sp.dma_start(vec_rows[at:at + KT, :], v.rearrange("(k p) -> k p", p=P)).then_inc(small_in, 16)
                sp.dma_start(bias_rows[:, i, :], bo[i].partition_broadcast(P)).then_inc(small_in, 16)
            sp.dma_start(vec_rows[6 * KT:NVEC, :], b_ff1.rearrange("(m p) -> m p", p=P)).then_inc(small_in, 16)

            def load_ctx(turn, s):
                sp.dma_start(cin[s][0:SK, 0:DC], ctx[turn * SLOTS + s]).then_inc(c_loaded[s], 16)
                sp.dma_start(cin[s][0:SK, DC:2 * P], ctx[turn * SLOTS + s, :, P:DC]).then_inc(c_loaded[s], 16)

            def load(turn):
                for s in range(SLOTS):
                    sp.dma_start(xin[s][:], x_view[turn * SLOTS + s]).then_inc(x_loaded[s], 16)
                    load_ctx(turn, s)

            load(0)
            for s in range(SLOTS):
                sp.sem_inc(stored[s], 16)
            sp.dma_start(ctx_all, ctx_view).then_inc(staged["ctx"], 16)
            for n in LOADS:
                if n in ("wo2", "ff1"):
                    sp.wait_ge(ctx_seen, 1)
                if n in view:
                    sp.dma_start(st(n), view[n]).then_inc(staged[n], 16)
                else:
                    sp.dma_start(st(n)[:, 0, :], w[n][0:P]).then_inc(staged[n], 16)
                    for at in (0, REST):
                        sp.dma_start(st(n)[at:at + REST, 1, :], w[n][P:DC]).then_inc(staged[n], 16)

            def store(turn):
                for s in range(SLOTS):
                    sp.wait_ge(result_ready, turn * SLOTS + s + 1 + SLOTS)
                    sp.dma_start(out_view[turn * SLOTS + s], xres[s][:]).then_inc(stored[s], 16)

            with sp.Fori(0, TURNS_OF_LOOP - 1) as turn:
                for s in range(SLOTS):
                    sp.wait_ge(x_biased[s], turn * 3 + 1)
                    sp.dma_start(xin[s][:], x_view[turn * SLOTS + SLOTS + s]).then_inc(x_loaded[s], 16)
                for s in range(SLOTS):
                    sp.wait_ge(group_full, group_of(turn, ("ctx", s)) + 1)
                    load_ctx(turn + 1, s)
                store(turn)
            for s in range(SLOTS):
                sp.sem_inc(x_loaded[s], 16)
            store(TURNS_OF_LOOP - 1)
            for s in range(SLOTS):
                sp.wait_ge(stored[s], 16 * TURNS_OF_LOOP + 16)

        @block.gpsimd
        def _(pool):
            nc.gpsimd.memset(ones[:], 1.0).then_inc(const_ready, 1)
            nc.gpsimd.memset(half[:], -0.5).then_inc(const_ready, 1)
            nc.gpsimd.memset(largest[:], 0.0).then_inc(const_ready, 1)
            nc.gpsimd.memset(ident[:], 0.0).then_inc(const_ready, 1)
            pool.wait_ge(const_ready, 4)
            nc.gpsimd.affine_select(out=ident[:], in_=ident[:], compare_op=ALU.not_equal, fill=1.0, base=0,
                                    pattern=[[-1, P]], channel_multiplier=1).then_inc(const_ready, 1)
            pool.wait_ge(const_ready, 5)
            pool.wait_ge(small_in, 16 * SMALL)

            def root(turn, s, n):
                i = ln_of(turn, s, n)
                pool.wait_ge(stats_ready, i + 1 + 1)
                pool.sem_inc(pool_past, 1)
                nc.gpsimd.tensor_scalar(spread[s][:, 0, :], moments[s][:, :, 1], EPS, None, ALU.add).then_inc(root_step, 1)
                pool.wait_ge(root_step, i + 1)
                nc.gpsimd.tensor_tensor(spread[s][:, 1, :], spread[s][:, 0, :], half[:], ALU.pow).then_inc(root_ready, 1)

            def add_bias(turn, s, n):
                rows = xin[s] if n == 1 else xres[s]
                if n == 1:
                    pool.wait_ge(stored[s], turn * 16 + 16)
                pool.wait_ge(xhat_ready, turn * NLN + LN_BEFORE[s, 1] + 1 if n == 1 else ln_of(turn, s, n) + 1)
                nc.gpsimd.tensor_tensor(xres[s][:], rows[:], bias_rows[:, n - 1:n, :].to_broadcast([P, TT, D]), ALU.add).then_inc(x_biased[s], 1)

            def normalise(turn, p):
                _, a, _ = of_pair(p)
                K = S if a == 1 else SK
                pool.wait_ge(share_ready, turn * NPAIR + p + 1)
                pool.sem_inc(pool_past, 1)
                for h in range(2):
                    for t in range(TT):
                        rows = probs[:, p % 4, h, t, 0:K]
                        nc.gpsimd.tensor_scalar(rows, rows, share[:, p % 4, 2 * h + t:2 * h + t + 1], 2.0 ** BOUND,
                                                ALU.mult, ALU.mult).then_inc(probs_ready, 1)

            for step in BEFORE:
                if step[0] == "stats":
                    root(None, *step[1:])
            for n in SPLIT:
                if n in LOW_BY_POOL:
                    pool.wait_ge(w_high, SPLIT.index(n) + 1)
                    pool.sem_inc(pool_past, 1)
                    nc.gpsimd.tensor_scalar(st(n), st(n), up[:, COL[n]:COL[n] + 1], None, ALU.mult).then_inc(scaled, 1)
                    pool.wait_ge(scaled, LOW_BY_POOL.index(n) + 1)
                    nc.gpsimd.tensor_tensor(wsb[n][:, 1], st(n), wsb[n][:, 0], ALU.subtract).then_inc(w_ready, 1)
                if n == "wo1":
                    pool.wait_ge(w2_ready, 1)
                    nc.gpsimd.tensor_tensor(w2sb[1][:], st("ff2"), w2sb[0][:].bitcast(F32), ALU.subtract).then_inc(w2_ready, 1)
            with pool.Fori(0, TURNS_OF_LOOP) as turn:
                for step in ORDER:
                    if step[0] == "stats":
                        root(turn, *step[1:])
                    elif step[0] == "bias":
                        add_bias(turn, step[1], 1)
                    elif step[0] == "rows" and step[2] > 1:
                        add_bias(turn, *step[1:])
                    elif step[0] == "norm":
                        normalise(turn, step[1])

        @block.scalar
        def _(act):
            for n in SPLIT:
                act.wait_ge(scales_ready, 1 if n in PHASES[0] else 2)
                act.wait_ge(staged[n], 16 if n in view else 48)
                nc.scalar.activation(wsb[n][:, 0], st(n), ACT.Copy, scale=up[:, COL[n]:COL[n] + 1]).then_inc(w_high, 1)
                if n == PHASES[0][-1]:
                    act.wait_ge(staged["ff2"], 16)
                    nc.scalar.activation(w2sb[0][:], st("ff2"), ACT.Copy).then_inc(w2_ready, 1)
            act.wait_ge(consts_ready, 1)

            def group(turn, step):
                act.wait_ge(group_full, group_of(turn, step) + 1)
                return group_ps[:, bank_of(turn, step), :]

            def h_halves(turn, s, n):
                act.wait_ge(group_done, group_of(turn, ("turn", s, n)) + 1 + RING)
                nc.scalar.activation(hT[s][:, 0], h32[:], ACT.Copy).then_inc(h_high, 1)

            def c_halves(turn, s):
                act.wait_ge(group_done, group_of(turn, ("ctx", s)) + 1 + RING)
                nc.scalar.activation(cT[s][:, 0], c32[:], ACT.Copy).then_inc(c_high, 1)

            def proj(turn, step):
                _, s, kind, j = step
                bank = group(turn, step)
                dst, src, shift_bits = proj_place(kind, s, j, bank, 0)
                nc.scalar.activation(dst, src, ACT.Copy, scale=2.0 ** -shift_bits).then_inc(group_high, 1)

            def exponentials(turn, p):
                _, a, _ = of_pair(p)
                K = S if a == 1 else SK
                act.wait_ge(shift_ready, turn * NPAIR + p + 1)
                for h in range(2):
                    for t in range(TT):
                        i = 2 * h + t
                        ins = nc.scalar.activation(probs[:, p % 4, h, t, 0:K], score_ps[:, p % 2, h, t * K:t * K + K], ACT.Exp,
                                                   scale=score_scale[a], bias=shift[:, p % 4, i:i + 1],
                                                   accum_out=total[:, p % 4, i:i + 1])
                ins.then_inc(exp_done, 1)

            def probs_high(turn, p):
                K = S if p < 2 * PAIRS else SK
                R = P if p < 2 * PAIRS else SK
                for u in units(p):
                    bank = group(turn, ("probs", u))
                    nc.scalar.activation(probsT[0:R, u % 4, 0, :], bank[0:R], ACT.Copy).then_inc(probsT_high, 1)

            def mix(turn, step):
                _, _, j = of_pair(step[1])
                bank = group(turn, step)
                nc.scalar.activation(mixed[:, 0, j, :], bank[:, 0:S], ACT.Copy, scale=2.0 ** -BOUND).then_inc(group_high, 1)

            def gated_done(turn, s, j):
                if s == A:
                    act.wait_ge(gated_ready, turn * FT + j + 1)
                else:
                    act.wait_ge(group_done, group_of(turn, ("ff1", s, j)) + 1 + RING)

            def gate(turn, step):
                _, s, j = step
                if s == A:
                    act.wait_ge(group_done, group_of(turn, ("ff1", s, j)) + 1 + RING)
                    src = raw[:, j, S:2 * S]
                else:
                    src = group(turn, ("ff1", s, j))[:, S:2 * S]
                if j >= 4:
                    gated_done(turn, s, j - 4)
                nc.scalar.activation(gelu[:, j % 4, :], src, ACT.Gelu, scale=ff_scale,
                                     bias=ffb[:, FT + j:FT + j + 1]).then_inc(gelu_done, 1)

            def inner_high_half(turn, step):
                _, s, i = step
                gated_done(turn, s, 2 * i + 1)
                act.wait_ge(inner_used, turn * (NTILE // 2) + s * (FT // 2) + i + 1)
                nc.scalar.activation(inner[0][:, 2 * i % 4:2 * i % 4 + 2, :], gated[:, 2 * i % 4:2 * i % 4 + 2, :], ACT.Copy).then_inc(inner_high, 1)

            for step in BEFORE:
                if step[0] == "turn":
                    h_halves(None, *step[1:])
            with act.Fori(0, TURNS_OF_LOOP) as turn:
                for step in ORDER:
                    if step[0] == "turn":
                        h_halves(turn, *step[1:])
                    elif step[0] == "ctx":
                        c_halves(turn, step[1])
                    elif step[0] == "proj":
                        proj(turn, step)
                    elif step[0] == "exp":
                        exponentials(turn, step[1])
                    elif step[0] == "probs":
                        probs_high(turn, step[1])
                    elif step[0] == "mix":
                        mix(turn, step)
                    elif step[0] == "gate":
                        gate(turn, step)
                    elif step[0] == "inner":
                        inner_high_half(turn, step)

        @block.vector
        def _(dve):
            count = [0]

            def link(ins):
                count[0] += 1
                ins.then_inc(setup, 1)
                dve.wait_ge(setup, count[0])

            dve.sem_inc(group_done, RING)
            dve.sem_inc(result_ready, SLOTS)
            dve.sem_inc(stats_ready, 1)
            dve.sem_inc(h_ready, 1)
            dve.sem_inc(inner_ready, 2)

            def stats(turn, s, n):
                i = ln_of(turn, s, n)
                if n == 1:
                    dve.wait_ge(x_loaded[s], 16 if turn is None else turn * 16 + 32)
                else:
                    last = max((("out", s, n - 1, t) for t in range(TT)), key=GROUP.get)
                    dve.wait_ge(group_done, group_of(turn, last) + 1 + RING)
                rows = xin[s] if n == 1 else xres[s]
                dve.wait_ge(stats_ready, i + 1)
                for t in range(TT):
                    ins = nc.vector.bn_stats(stat6[:, t, :], rows[:, t, :])
                ins.then_inc(stat_step, 1)
                dve.wait_ge(stat_step, i + 1)
                dve.sem_inc(dve_past, 1)
                for t in range(TT):
                    ins = nc.vector.bn_aggr(moments[s][:, t, :], stat6[:, t, :])
                ins.then_inc(stats_ready, 1)

            def normal_rows(turn, s, n):
                dve.wait_ge(root_ready, ln_of(turn, s, n) + 1)
                rows = xin[s] if n == 1 else xres[s]
                for t in range(TT):
                    ins = nc.vector.tensor_scalar(xhat[s][:, t, :], rows[:, t, :], moments[s][:, t, 0:1], spread[s][:, 1, t:t + 1],
                                                  ALU.subtract, ALU.mult)
                ins.then_inc(xhat_ready, 1)

            for step in BEFORE:
                if step[0] == "stats":
                    stats(None, *step[1:])
                elif step[0] == "rows":
                    normal_rows(None, *step[1:])
            dve.wait_ge(const_ready, 5)
            dve.wait_ge(vecs_turned, 1)
            link(nc.vector.tensor_copy(vecs[:], group_ps[:, 1, 0:NVEC]))
            for i in range(3):
                for c, n in enumerate(("h", "b")):
                    k = COL[f"{n}{i + 1}"]
                    link(nc.vector.tensor_reduce(largest[:, k:k + 1], gains[:, i, c, :], AX.X, ALU.max, apply_absolute_value=True))
            dve.wait_ge(staged["ctx"], 16)
            nc.vector.tensor_reduce(largest[:, COL["ctx"]:COL["ctx"] + 1], ctx_all, AX.X, ALU.max, apply_absolute_value=True).then_inc(ctx_seen, 1)

            def find_scales(phase):
                for n in PHASES[phase]:
                    dve.wait_ge(staged[n], 16 if n in view else 48)
                    link(nc.vector.tensor_reduce(largest[:, COL[n]:COL[n] + 1], st(n), AX.XY, ALU.max, apply_absolute_value=True))
                dve.wait_ge(ctx_seen, 1)
                dve.sem_inc(largest_ready, 1)
                a, z = COLUMNS[phase]
                dve.wait_ge(turned, phase + 1)
                link(nc.vector.tensor_reduce(top[0:z - a], group_ps[0:z - a, 0, 0:P], AX.X, ALU.max))
                nc.vector.tensor_scalar(diag[0:z - a, 0:z - a], ident[0:z - a, 0:z - a], top[0:z - a, 0:1], None, ALU.mult).then_inc(diag_ready, 1)
                dve.wait_ge(spread_out, phase + 1)
                link(nc.vector.tensor_copy(bound[:, a:z], group_ps[:, 1, 0:z - a]))
                if phase == 1:
                    h, hb = COL["h1"], COL["b1"]
                    link(nc.vector.tensor_tensor(bound[:, h:h + 3], bound[:, h:h + 3], bound[:, hb:hb + 3], ALU.add))
                    link(nc.vector.tensor_scalar(bound[:, h:h + 3], bound[:, h:h + 3], float(D) ** 0.5, None, ALU.mult))
                link(nc.vector.tensor_scalar(bound[:, a:z], bound[:, a:z], FLOOR, None, ALU.max))
                link(nc.vector.tensor_scalar(power[:, a:z].bitcast(I32), bound[:, a:z].bitcast(I32), EXPONENT, None, ALU.bitwise_and))
                link(nc.vector.reciprocal(up[:, a:z], power[:, a:z]))
                link(nc.vector.tensor_scalar(up[:, a:z], up[:, a:z], 2.0 ** (BOUND - 1), None, ALU.mult))
                dve.sem_inc(scales_ready, 1)
                link(nc.vector.tensor_scalar(down[:, a:z], power[:, a:z], 2.0 ** (1 - BOUND), None, ALU.mult))

            def low_halves(phase):
                for n in PHASES[phase]:
                    if n not in LOW_BY_POOL:
                        dve.wait_ge(w_high, SPLIT.index(n) + 1)
                        nc.vector.scalar_tensor_tensor(wsb[n][:, 1], st(n), up[:, COL[n]:COL[n] + 1], wsb[n][:, 0],
                                                       ALU.mult, ALU.subtract).then_inc(w_ready, 1)

            find_scales(0)
            low_halves(0)
            find_scales(1)

            def times(dst, one, two, factor):
                link(nc.vector.scalar_tensor_tensor(dst, one, factor, two, ALU.mult, ALU.mult))

            def d(n):
                return down[:, COL[n]:COL[n] + 1]

            def u(n):
                return up[:, COL[n]:COL[n] + 1]

            times(part[:, 0:1], d("h1"), d("wq1"), 2.0 ** Q_SHIFT)
            times(part[:, 1:2], d("h1"), d("wk1"), 2.0 ** Q_SHIFT)
            times(score_scale[1], part[:, 0:1], part[:, 1:2], SCALE)
            times(part[:, 2:3], d("h2"), d("wq2"), 2.0 ** Q_SHIFT)
            times(part[:, 3:4], d("ctx"), d("wk2"), 2.0 ** C_SHIFT)
            times(score_scale[2], part[:, 2:3], part[:, 3:4], SCALE)
            for a in (1, 2):
                link(nc.vector.tensor_scalar(score_minus[a], score_scale[a], -1.0, None, ALU.mult))
            times(part[:, 0:1], d("h1"), d("wv1"), 2.0 ** Q_SHIFT)
            times(out_scale[1], part[:, 0:1], d("wo1"), 1.0)
            times(part[:, 1:2], d("ctx"), d("wv2"), 2.0 ** C_SHIFT)
            times(out_scale[2], part[:, 1:2], d("wo2"), 1.0)
            times(ff_scale, d("h3"), d("ff1"), 1.0)
            times(ff_up, u("h3"), u("ff1"), 1.0)
            link(nc.vector.tensor_scalar(ffb_a[:], ffb[:, 0:FT], ff_up, None, ALU.mult))
            for i in range(3):
                link(nc.vector.tensor_scalar(gains_s[:, i], gains[:, i], u(f"h{i + 1}"), None, ALU.mult))
            dve.sem_inc(consts_ready, 1)
            low_halves(1)
            dve.wait_ge(w_ready, len(WEIGHTS))
            dve.wait_ge(w2_ready, 2)

            def group(turn, step):
                dve.wait_ge(group_full, group_of(turn, step) + 1)
                return group_ps[:, bank_of(turn, step), :]

            def h_halves(turn, step):
                _, s, n = step
                dve.wait_ge(h_ready, ln_of(turn, s, n) + 1)
                bank = group(turn, step)
                for k in range(KT):
                    ins = nc.vector.tensor_scalar(h32[:, k, :], bank[:, k * S:k * S + S], gains_s[:, n - 1, 0, k:k + 1],
                                                  gains_s[:, n - 1, 1, k:k + 1], ALU.mult, ALU.add)
                ins.then_inc(group_done, 1)
                dve.wait_ge(h_high, ln_of(turn, s, n) + 1)
                nc.vector.tensor_tensor(hT[s][:, 1], h32[:], hT[s][:, 0], ALU.subtract).then_inc(h_ready, 1)

            def c_halves(turn, step):
                _, s = step
                bank = group(turn, step)
                nc.vector.tensor_scalar(c32[:], bank[:, 0:2 * SK].rearrange("p (k n) -> p k n", k=2), u("ctx"), None,
                                        ALU.mult).then_inc(group_done, 1)
                dve.wait_ge(c_high, turn * SLOTS + CTXS[s] + 1)
                nc.vector.tensor_tensor(cT[s][:, 1, 0], c32[:, 0], cT[s][:, 0, 0], ALU.subtract)
                rest = cT[s][REST:P, 0, 1]
                nc.vector.tensor_tensor(rest, c32[REST:P, 1], rest, ALU.subtract).then_inc(c_ready, 1)

            def low(turn, step, dst, src, high, factor):
                dve.wait_ge(group_high, turn * NHIGH + HIGH[step] + 1)
                nc.vector.scalar_tensor_tensor(dst, src, factor, high, ALU.mult, ALU.subtract).then_inc(group_done, 1)

            def proj(turn, step):
                _, s, kind, j = step
                bank = group_ps[:, bank_of(turn, step), :]
                high, src, shift_bits = proj_place(kind, s, j, bank, 0)
                dst, _, _ = proj_place(kind, s, j, bank, 1)
                low(turn, step, dst, src, high, 2.0 ** -shift_bits)

            def mix(turn, step):
                _, _, j = of_pair(step[1])
                low(turn, step, mixed[:, 1, j, :], group_ps[:, bank_of(turn, step), 0:S], mixed[:, 0, j, :], 2.0 ** -BOUND)

            def maxima(turn, p):
                _, a, _ = of_pair(p)
                K = S if a == 1 else SK
                dve.wait_ge(scores_full, turn * NPAIR + p + 1)
                nc.vector.tensor_reduce(peak[:, p % 4, :].rearrange("p (h t) -> p h t", h=2),
                                        score_ps[:, p % 2, :, 0:TT * K].rearrange("p h (t k) -> p h t k", t=TT),
                                        AX.X, ALU.max).then_inc(peak_ready, 1)
                dve.wait_ge(peak_ready, turn * NPAIR + p + 1)
                nc.vector.tensor_scalar(shift[:, p % 4, :], peak[:, p % 4, :], score_minus[a], None, ALU.mult).then_inc(shift_ready, 1)

            def shares(turn, p):
                dve.wait_ge(exp_done, turn * NPAIR + p + 1)
                nc.vector.reciprocal(share[:, p % 4, :], total[:, p % 4, :]).then_inc(share_ready, 1)

            def probs_low(turn, p):
                R = P if p < 2 * PAIRS else SK
                for unit in units(p):
                    dve.wait_ge(probsT_high, turn * NUNIT + unit + 1)
                    bank = group_ps[:, bank_of(turn, ("probs", unit)), :]
                    nc.vector.tensor_tensor(probsT[0:R, unit % 4, 1, :], bank[0:R], probsT[0:R, unit % 4, 0, :],
                                            ALU.subtract).then_inc(group_done, 1)

            def residual(turn, step):
                _, s, n, t = step
                bank = group(turn, step)
                dve.wait_ge(x_biased[s], turn * 3 + n)
                nc.vector.scalar_tensor_tensor(xres[s][:, t, :], bank[:, 0:D], out_scale[n], xres[s][:, t, :],
                                               ALU.mult, ALU.add).then_inc(group_done, 1)

            def keep_products(turn, step):
                _, s, j = step
                bank = group(turn, step)
                nc.vector.tensor_copy(raw[:, j, :], bank).then_inc(group_done, 1)

            def gate(turn, step):
                _, s, j = step
                pairs_before = turn * (NTILE // 2) + s * (FT // 2) + j // 2
                dve.wait_ge(inner_ready, pairs_before + 1)
                dve.wait_ge(gelu_done, turn * NTILE + s * FT + j + 1)
                src, done = (raw[:, j, 0:S], gated_ready) if s == A else (group_ps[:, bank_of(turn, ("ff1", s, j)), 0:S], group_done)
                nc.vector.scalar_tensor_tensor(gated[:, j % 4, :], src, ffb_a[:, j:j + 1], gelu[:, j % 4, :],
                                               ALU.add, ALU.mult).then_inc(done, 1)

            def inner_low_half(turn, step):
                _, s, i = step
                dve.wait_ge(inner_high, turn * (NTILE // 2) + s * (FT // 2) + i + 1)
                two = slice(2 * i % 4, 2 * i % 4 + 2)
                nc.vector.tensor_tensor(inner[1][:, two, :], gated[:, two, :], inner[0][:, two, :].bitcast(F32),
                                        ALU.subtract).then_inc(inner_ready, 1)

            def finish(turn, s):
                dve.wait_ge(inner_used, turn * (NTILE // 2) + (s + 1) * (FT // 2) + 2)
                dve.wait_ge(x_biased[s], turn * 3 + 3)
                ins = nc.vector.scalar_tensor_tensor(xres[s][:], score_ps[:, s, :, 0:D], ff_scale, xres[s][:], ALU.mult, ALU.add)
                ins.then_inc(result_ready, 1)

            for step in BEFORE:
                if step[0] == "turn":
                    h_halves(None, step)
            with dve.Fori(0, TURNS_OF_LOOP) as turn:
                for step in ORDER:
                    if step[0] == "stats":
                        stats(turn, *step[1:])
                    elif step[0] == "rows":
                        normal_rows(turn, *step[1:])
                    elif step[0] == "turn":
                        h_halves(turn, step)
                    elif step[0] == "ctx":
                        c_halves(turn, step)
                    elif step[0] == "proj":
                        proj(turn, step)
                    elif step[0] == "max":
                        maxima(turn, step[1])
                    elif step[0] == "share":
                        shares(turn, step[1])
                    elif step[0] == "probs":
                        probs_low(turn, step[1])
                    elif step[0] == "mix":
                        mix(turn, step)
                    elif step[0] == "out":
                        residual(turn, step)
                    elif step[0] == "ff1" and step[1] == A:
                        keep_products(turn, step)
                    elif step[0] == "gate":
                        gate(turn, step)
                    elif step[0] == "inner":
                        inner_low_half(turn, step)
                    elif step[0] == "finish":
                        finish(turn, step[1])

        @block.tensor
        def _(pe):
            pe.wait_ge(const_ready, 5)
            pe.wait_ge(small_in, 16 * SMALL)
            nc.tensor.transpose(group_ps[:, 1, 0:NVEC], vec_rows[:], ident[0:NVEC, 0:NVEC]).then_inc(vecs_turned, 1)
            for phase, (a, z) in enumerate(COLUMNS):
                pe.wait_ge(largest_ready, phase + 1)
                nc.tensor.transpose(group_ps[0:z - a, 0, 0:P], largest[:, a:z], ident[:]).then_inc(turned, 1)
                pe.wait_ge(diag_ready, phase + 1)
                nc.tensor.matmul(group_ps[:, 1, 0:z - a], ones[0:z - a], diag[0:z - a, 0:z - a], start=True, stop=True).then_inc(spread_out, 1)
            pe.wait_ge(w_ready, len(WEIGHTS))
            pe.wait_ge(w2_ready, 2)
            pe.sem_inc(inner_used, 2)

            def done(turn, *steps):
                pe.wait_ge(group_done, group_of(turn, max(steps, key=GROUP.get)) + 1 + RING)

            def group(turn, step, *after):
                if max([GROUP[x] + RING for x in after], default=-1) > GROUP.get(step, 0):
                    done(turn, *after)
                else:
                    pe.wait_ge(group_done, group_of(turn, step) + 1)
                return group_ps[:, bank_of(turn, step), :]

            def turn_rows(turn, step):
                _, s, n = step
                pe.wait_ge(xhat_ready, ln_of(turn, s, n) + 1)
                bank = group(turn, step)
                for k in range(KT):
                    for t in range(TT):
                        ins = nc.tensor.transpose(bank[:, k * S + t * P:k * S + t * P + P], xhat[s][:, t, k * P:k * P + P], ident[:])
                ins.then_inc(group_full, 1)

            def turn_ctx(turn, step):
                _, s = step
                pe.wait_ge(c_loaded[s], turn * 32 + 32)
                bank = group(turn, step)
                for k in range(2):
                    ins = nc.tensor.transpose(bank[:, k * SK:k * SK + SK], cin[s][0:SK, k * P:k * P + P], ident[0:SK, 0:SK])
                ins.then_inc(group_full, 1)

            def proj(turn, step):
                _, s, kind, j = step
                if kind[1] == "1":
                    pe.wait_ge(h_ready, turn * NLN + LN_BEFORE[s, 1] + 2)
                elif kind == "q2":
                    pe.wait_ge(h_ready, ln_of(turn, s, 2) + 2)
                else:
                    pe.wait_ge(c_ready, turn * SLOTS + CTXS[s] + 1)
                bank = group(turn, step)
                name = "w" + kind
                products = CTX_PRODUCTS if kind in ("k2", "v2") else [(a, z, k, P) for k in range(KT) for a, z in THREE]
                src = cT[s] if kind in ("k2", "v2") else hT[s]
                last = len(products) - 1
                if kind in ("q1", "k1", "q2", "k2"):
                    n, per = (SK, 4) if kind == "k2" else (S, 2)
                    for m in range(per):
                        at = (per * j + m) * P
                        for i, (a, z, k, rows) in enumerate(products):
                            ins = nc.tensor.matmul(bank[:, m * n:m * n + n], weight(name, z, k, at, at + P, rows), src[0:rows, a, k, :],
                                                   start=(i == 0), stop=(i == last))
                else:
                    t, c, M = (j // 2, j % 2, P) if kind == "v1" else (0, j, SK)
                    for i, (a, z, k, rows) in enumerate(products):
                        ins = nc.tensor.matmul(bank[0:M], src[0:rows, a, k, t * P:t * P + M], weight(name, z, k, c * 512, c * 512 + 512, rows),
                                               start=(i == 0), stop=(i == last))
                ins.then_inc(group_full, 1)

            def scores(turn, p):
                s, a, j = of_pair(p)
                done(turn, ("proj", s, f"q{a}", j // 2), ("proj", s, f"k{a}", j // 2 if a == 1 else j // 4))
                if p < 2:
                    pe.wait_ge(result_ready, turn * SLOTS + p + 1)
                else:
                    pe.wait_ge(exp_done, turn * NPAIR + p - 1)
                K = S if a == 1 else SK
                q, k = qkv[s, "q"], qkv[s, "k"]
                for t in range(TT):
                    for i, (a_, z) in enumerate(THREE):
                        for h in range(2):
                            r = slice(h * DH, h * DH + DH)
                            ins = nc.tensor.matmul(score_ps[:, p % 2, h, t * K:t * K + K], q[r, a_, j, t * P:t * P + P], k[r, z, j, 0:K],
                                                   start=(i == 0), stop=(i == 2))
                ins.then_inc(scores_full, 1)

            def turn_probs(turn, p):
                _, a, _ = of_pair(p)
                pe.wait_ge(probs_ready, turn * (4 * NPAIR) + 4 * (p + 1))
                for h in range(2):
                    u = units(p)[h if a == 1 else 0]
                    if a == 1 or h == 0:
                        bank = group(turn, ("probs", u))
                    for k in range(TT if a == 1 else 1):
                        K = P if a == 1 else SK
                        for t in range(TT):
                            at = (k if a == 1 else h) * S + t * P
                            ins = nc.tensor.transpose(bank[0:K, at:at + P], probs[:, p % 4, h, t, k * P:k * P + K], ident[:])
                    if a == 1 or h == 1:
                        ins.then_inc(group_full, 1)

            def mix(turn, step):
                p = step[1]
                s, a, j = of_pair(p)
                values = [("proj", s, "v1", j // 4), ("proj", s, "v1", 2 + j // 4)] if a == 1 else [("proj", s, "v2", j // 4)]
                bank = group(turn, step, ("probs", units(p)[-1]), *values)
                v = qkv[s, "v"]
                kts = TT if a == 1 else 1
                K = P if a == 1 else SK
                for k in range(kts):
                    for i, (a_, z) in enumerate(THREE):
                        for h in range(2):
                            u = units(p)[h if a == 1 else 0]
                            at = (k if a == 1 else h) * S
                            ins = nc.tensor.matmul(bank[h * DH:h * DH + DH, 0:S], v[0:K, z, k, (2 * j + h) * DH:(2 * j + h + 1) * DH],
                                                   probsT[0:K, u % 4, a_, at:at + S], start=(k == 0 and i == 0), stop=(k == kts - 1 and i == 2))
                ins.then_inc(group_full, 1)

            def project_out(turn, step):
                _, s, n, t = step
                last = (n - 1) * 2 * PAIRS + s * PAIRS + PAIRS - 1
                bank = group(turn, step, ("mix", last))
                for c in range(AT):
                    for i, (a, z) in enumerate(THREE):
                        ins = nc.tensor.matmul(bank[:, 0:D], mixed[:, a, c, t * P:t * P + P], wsb[f"wo{n}"][:, z, c, :],
                                               start=(c == 0 and i == 0), stop=(c == AT - 1 and i == 2))
                ins.then_inc(group_full, 1)

            def ff1(turn, step):
                _, s, j = step
                pe.wait_ge(h_ready, ln_of(turn, s, 3) + 2)
                bank = group(turn, step)
                for half_ in (1, 0):
                    at = half_ * FF + j * P
                    for k in range(KT):
                        for i, (a, z) in enumerate(THREE):
                            ins = nc.tensor.matmul(bank[:, half_ * S:half_ * S + S], weight("ff1", z, k, at, at + P), hT[s][:, a, k, :],
                                                   start=(k == 0 and i == 0), stop=(k == KT - 1 and i == 2))
                ins.then_inc(group_full, 1)

            def ff2(turn, step):
                _, s, j = step
                if j == 0:
                    pe.wait_ge(exp_done, turn * NPAIR + NPAIR - 1 + s)
                pe.wait_ge(inner_ready, turn * (NTILE // 2) + s * (FT // 2) + j // 2 + 1 + 2)
                for t in range(TT):
                    for i, (a, z) in enumerate(THREE):
                        ins = nc.tensor.matmul(score_ps[:, s, t, 0:D], inner[a][:, j % 4, t * P:t * P + P], w2sb[z][:, j, :],
                                               start=(j == 0 and i == 0), stop=(j == FT - 1 and i == 2))
                if j % 2:
                    ins.then_inc(inner_used, 1)

            for step in BEFORE:
                if step[0] == "turn":
                    turn_rows(None, step)
            with pe.Fori(0, TURNS_OF_LOOP) as turn:
                for step in ORDER:
                    if step[0] == "turn":
                        turn_rows(turn, step)
                    elif step[0] == "ctx":
                        turn_ctx(turn, step)
                    elif step[0] == "proj":
                        proj(turn, step)
                    elif step[0] == "scores":
                        scores(turn, step[1])
                    elif step[0] == "probs":
                        turn_probs(turn, step[1])
                    elif step[0] == "mix":
                        mix(turn, step)
                    elif step[0] == "out":
                        project_out(turn, step)
                    elif step[0] == "ff1":
                        ff1(turn, step)
                    elif step[0] == "ff2":
                        ff2(turn, step)


def kernel(**inputs):
    import numpy as np
    import concourse.bacc as bacc
    from concourse.bass_utils import run_bass_kernel_spmd

    nc = bacc.Bacc("TRN2", target_bir_lowering=False, num_devices=1, dynamic_dma_scratch_size=2048)
    arrays, aps = {}, {}
    for name, value in inputs.items():
        array = np.ascontiguousarray(value)
        arrays[f"in_{name}"] = array
        aps[name] = nc.dram_tensor(f"in_{name}", array.shape, mybir.dt.from_np(array.dtype), kind="ExternalInput").ap()
    shape = inputs["x"].shape
    out = nc.dram_tensor("out", shape, F32, kind="ExternalOutput").ap()

    def of(name):
        return aps["L0_xattn_" + name]

    w = {n: of(n) for n in WEIGHTS if n != "ff1"}
    w["ff1"], w["ff2"] = of("w_ff1"), of("w_ff2")
    bass_xattn_block(nc, aps["x"], aps["ctx_768"], w, [of(f"g{i}") for i in (1, 2, 3)], [of(f"b{i}") for i in (1, 2, 3)],
                     [of("bo1"), of("bo2"), of("b_ff2")], of("b_ff1"), out)
    result = run_bass_kernel_spmd(nc, [arrays], core_ids=[0])
    return result.results[0]["out"]
```
